# Optimizing a Trainium2 kernel written in Bass

```python
import numpy as np
import jax
import jax.numpy as jnp

def _softmax(x, axis=-1):
    return jax.nn.softmax(x, axis=axis)

def _gelu(x):
    return jax.nn.gelu(x, approximate=True)

def _silu(x):
    return jax.nn.silu(x)

def _sigmoid(x):
    return jax.nn.sigmoid(x)

def _layernorm(x, axis=-1, eps=1e-05):
    m = jnp.mean(x, axis=axis, keepdims=True)
    v = jnp.var(x, axis=axis, keepdims=True)
    return (x - m) / jnp.sqrt(v + eps)

def _scatter_add(tgt, idx, src, axis=0):
    return tgt.at[idx].add(src)

def _segment_sum(src, seg, n):
    return jax.ops.segment_sum(src, seg, n)
kernel_name = 'mk_gnn_resnorm_d4_gnn_r8_66adf8'

def setup_inputs(seed: int=0):
    np.random.seed(seed)
    _w = jnp.asarray

    def _rec_inputs():
        import jax
        import jax.numpy as jnp
        _gk = jax.random.key(seed)
        x = -0.0005121 + 1.001 * jax.random.normal(jax.random.fold_in(_gk, 1), (6250, 64), jnp.float32)
        _s = jax.random.randint(jax.random.fold_in(_gk, 2), (100000,), 0, 6250, jnp.int32)
        _d = jax.random.randint(jax.random.fold_in(_gk, 3), (100000,), 0, 6250, jnp.int32)
        _loop = jnp.arange(6250, dtype=jnp.int32)
        src = jnp.concatenate([_s, _d, _loop])
        dst = jnp.concatenate([_d, _s, _loop])
        _o = jnp.argsort(dst, stable=True)
        src = src[_o]
        dst = dst[_o]
        edge_attr_16 = 0.000196303 + 1.00016 * jax.random.normal(jax.random.fold_in(_gk, 11), (206250, 16), jnp.float32)
        edge_attr_64 = 4.59472e-05 + 1.00006 * jax.random.normal(jax.random.fold_in(_gk, 12), (206250, 64), jnp.float32)
        edge_weight = jax.random.uniform(jax.random.fold_in(_gk, 14), (206250,), jnp.float32, 0.0, 0.999998)
        return (x, src, dst, edge_attr_16, edge_attr_64, edge_weight)
    x, src, dst, edge_attr_16, edge_attr_64, edge_weight = _rec_inputs()

    def _L0_gnn_setup():
        import jax, jax.numpy as jnp
        import numpy as np
        N, E, D, EA = (6250, 200000, 64, 16)

        def _glorot(key, shape):
            fan_in, fan_out = (shape[0], shape[1])
            lim = (6.0 / (fan_in + fan_out)) ** 0.5
            return jax.random.uniform(key, shape, jnp.float32, -lim, lim)

        def _sage_conv(x, src, dst, ea, Wl, bl, Wr):
            msg = jax.nn.relu(x[src] + ea)
            s = jax.ops.segment_sum(msg, dst, num_segments=N)
            cnt = jax.ops.segment_sum(jnp.ones((msg.shape[0],), msg.dtype), dst, num_segments=N)
            agg = s / jnp.maximum(cnt, 1.0)[:, None]
            return agg @ Wl + bl + x @ Wr
        key = jax.random.key(seed)
        ks = jax.random.split(key, 16)
        inp = {'x': jax.random.normal(ks[0], (N, D), jnp.float32), 'edge_index': jax.random.randint(ks[1], (2, E), 0, N, jnp.int32), 'edge_attr': jax.random.normal(ks[2], (E, EA), jnp.float32), 'emb_ea': jax.random.normal(ks[3], (EA, D), jnp.float32)}
        for i in range(3):
            inp[f'Wl{i}'] = _glorot(ks[4 + 3 * i], (D, D))
            inp[f'bl{i}'] = jnp.zeros((D,), jnp.float32)
            inp[f'Wr{i}'] = _glorot(ks[5 + 3 * i], (D, D))
        return inp
    _L0_gnn_all = _L0_gnn_setup()
    _L0_gnn_in = {k: v for k, v in _L0_gnn_all.items() if k in ('emb_ea', 'Wl0', 'bl0', 'Wr0', 'Wl1', 'bl1', 'Wr1', 'Wl2', 'bl2', 'Wr2')}
    del _L0_gnn_all

    def _L1_gnn_setup():
        import jax, jax.numpy as jnp
        import numpy as np
        N_NODES = 6250
        N_EDGES = 100000
        D = 64

        def _wgin_layer(x, src, dst, edge_weight, W1, W2):
            msg = edge_weight[:, None] * x[src]
            agg = jax.ops.segment_sum(msg, dst, num_segments=x.shape[0])
            h = jax.nn.relu(agg @ W1.T)
            return h @ W2.T
        key = jax.random.key(seed)
        ks = jax.random.split(key, 7)
        x = jax.random.normal(ks[0], (N_NODES, D), dtype=jnp.float32)
        edge_index = jax.random.randint(ks[1], (2, N_EDGES), 0, N_NODES, dtype=jnp.int64)
        edge_weight = jax.random.uniform(ks[2], (N_EDGES,), dtype=jnp.float32)
        scale = 1.0 / np.sqrt(D)
        W1_0 = jax.random.normal(ks[3], (D, D), dtype=jnp.float32) * scale
        W2_0 = jax.random.normal(ks[4], (D, D), dtype=jnp.float32) * scale
        W1_1 = jax.random.normal(ks[5], (D, D), dtype=jnp.float32) * scale
        W2_1 = jax.random.normal(ks[6], (D, D), dtype=jnp.float32) * scale
        return {'x': x, 'edge_index': edge_index, 'edge_weight': edge_weight, 'W1_0': W1_0, 'W2_0': W2_0, 'W1_1': W1_1, 'W2_1': W2_1}
    _L1_gnn_all = _L1_gnn_setup()
    _L1_gnn_in = {k: v for k, v in _L1_gnn_all.items() if k in ('W1_0', 'W2_0', 'W1_1', 'W2_1')}
    del _L1_gnn_all

    def _L2_gnn_setup():
        import jax, jax.numpy as jnp
        import numpy as np
        N_NODES = 12500
        key = jax.random.key(seed)
        k1, k2, k3 = jax.random.split(key, 3)
        E, D = (156250, 64)
        edge_index = jax.random.randint(k1, (2, E), 0, N_NODES, dtype=jnp.int64)
        x = jax.random.normal(k2, (N_NODES, D), dtype=jnp.float32)
        W = jax.random.normal(k3, (E, D), dtype=jnp.float32)
        return {'edge_index': edge_index, 'x': x, 'W': W}
    _L2_gnn_all = _L2_gnn_setup()
    _L2_gnn_in = {k: v for k, v in _L2_gnn_all.items() if k in ()}
    del _L2_gnn_all

    def _L3_gnn_setup():
        import jax, jax.numpy as jnp
        import numpy as np
        H, C = (8, 8)
        NEG_SLOPE = 0.2

        def _leaky_relu(x):
            return jnp.where(x > 0, x, NEG_SLOPE * x)

        def _gat_layer(x, src, dst, W, a_src, a_dst, b):
            N = x.shape[0]
            h = (x @ W.T).reshape(N, H, C)
            alpha_s = jnp.einsum('nhc,hc->nh', h, a_src)
            alpha_d = jnp.einsum('nhc,hc->nh', h, a_dst)
            e = _leaky_relu(alpha_s[src] + alpha_d[dst])
            e_max = jax.ops.segment_max(e, dst, num_segments=N)
            e_exp = jnp.exp(e - e_max[dst])
            denom = jax.ops.segment_sum(e_exp, dst, num_segments=N)
            alpha = e_exp / denom[dst]
            msg = alpha[:, :, None] * h[src]
            out = jax.ops.segment_sum(msg, dst, num_segments=N)
            return out.reshape(N, H * C) + b
        key = jax.random.key(seed)
        ks = jax.random.split(key, 14)
        N, E = (12500, 200000)
        inp = {'x': jax.random.normal(ks[0], (N, 64), dtype=jnp.float32), 'edge_index': jax.random.randint(ks[1], (2, E), 0, N, dtype=jnp.int64)}
        s = 0.1
        for i, tag in enumerate(['1', '2', '3']):
            k0, k1, k2 = (ks[2 + 4 * i], ks[3 + 4 * i], ks[4 + 4 * i])
            inp['W' + tag] = jax.random.normal(k0, (H * C, 64), dtype=jnp.float32) * s
            inp['as' + tag] = jax.random.normal(k1, (H, C), dtype=jnp.float32) * s
            inp['ad' + tag] = jax.random.normal(k2, (H, C), dtype=jnp.float32) * s
            inp['b' + tag] = jnp.zeros((H * C,), dtype=jnp.float32)
        return inp
    _L3_gnn_all = _L3_gnn_setup()
    _L3_gnn_in = {k: v for k, v in _L3_gnn_all.items() if k in ('W1', 'as1', 'ad1', 'b1', 'W2', 'as2', 'ad2', 'b2', 'W3', 'as3', 'ad3', 'b3')}
    del _L3_gnn_all
    return {'x': x, 'src': src, 'dst': dst, 'edge_attr_16': edge_attr_16, 'edge_attr_64': edge_attr_64, 'edge_weight': edge_weight, 'L0_gnn_emb_ea': _L0_gnn_in['emb_ea'], 'L0_gnn_Wl0': _L0_gnn_in['Wl0'], 'L0_gnn_bl0': _L0_gnn_in['bl0'], 'L0_gnn_Wr0': _L0_gnn_in['Wr0'], 'L0_gnn_Wl1': _L0_gnn_in['Wl1'], 'L0_gnn_bl1': _L0_gnn_in['bl1'], 'L0_gnn_Wr1': _L0_gnn_in['Wr1'], 'L0_gnn_Wl2': _L0_gnn_in['Wl2'], 'L0_gnn_bl2': _L0_gnn_in['bl2'], 'L0_gnn_Wr2': _L0_gnn_in['Wr2'], 'L1_gnn_W1_0': _L1_gnn_in['W1_0'], 'L1_gnn_W2_0': _L1_gnn_in['W2_0'], 'L1_gnn_W1_1': _L1_gnn_in['W1_1'], 'L1_gnn_W2_1': _L1_gnn_in['W2_1'], 'L3_gnn_W1': _L3_gnn_in['W1'], 'L3_gnn_as1': _L3_gnn_in['as1'], 'L3_gnn_ad1': _L3_gnn_in['ad1'], 'L3_gnn_b1': _L3_gnn_in['b1'], 'L3_gnn_W2': _L3_gnn_in['W2'], 'L3_gnn_as2': _L3_gnn_in['as2'], 'L3_gnn_ad2': _L3_gnn_in['ad2'], 'L3_gnn_b2': _L3_gnn_in['b2'], 'L3_gnn_W3': _L3_gnn_in['W3'], 'L3_gnn_as3': _L3_gnn_in['as3'], 'L3_gnn_ad3': _L3_gnn_in['ad3'], 'L3_gnn_b3': _L3_gnn_in['b3']}

def reference(x, src, dst, edge_attr_16, edge_attr_64, edge_weight, L0_gnn_emb_ea, L0_gnn_Wl0, L0_gnn_bl0, L0_gnn_Wr0, L0_gnn_Wl1, L0_gnn_bl1, L0_gnn_Wr1, L0_gnn_Wl2, L0_gnn_bl2, L0_gnn_Wr2, L1_gnn_W1_0, L1_gnn_W2_0, L1_gnn_W1_1, L1_gnn_W2_1, L3_gnn_W1, L3_gnn_as1, L3_gnn_ad1, L3_gnn_b1, L3_gnn_W2, L3_gnn_as2, L3_gnn_ad2, L3_gnn_b2, L3_gnn_W3, L3_gnn_as3, L3_gnn_ad3, L3_gnn_b3):
    import jax
    import jax.numpy as jnp

    def _L0_gnn_ref(x, edge_index, edge_attr, emb_ea, Wl0, bl0, Wr0, Wl1, bl1, Wr1, Wl2, bl2, Wr2):
        import jax, jax.numpy as jnp
        import numpy as np
        N, E, D, EA = (6250, 200000, 64, 16)

        def _glorot(key, shape):
            fan_in, fan_out = (shape[0], shape[1])
            lim = (6.0 / (fan_in + fan_out)) ** 0.5
            return jax.random.uniform(key, shape, jnp.float32, -lim, lim)

        def _sage_conv(x, src, dst, ea, Wl, bl, Wr):
            msg = jax.nn.relu(x[src] + ea)
            s = jax.ops.segment_sum(msg, dst, num_segments=N)
            cnt = jax.ops.segment_sum(jnp.ones((msg.shape[0],), msg.dtype), dst, num_segments=N)
            agg = s / jnp.maximum(cnt, 1.0)[:, None]
            return agg @ Wl + bl + x @ Wr
        src, dst = (edge_index[0], edge_index[1])
        ea = edge_attr @ emb_ea
        x = jax.nn.relu(_sage_conv(x, src, dst, ea, Wl0, bl0, Wr0))
        x = jax.nn.relu(_sage_conv(x, src, dst, ea, Wl1, bl1, Wr1))
        x = _sage_conv(x, src, dst, ea, Wl2, bl2, Wr2)
        return x

    def _L1_gnn_ref(x, edge_index, edge_weight, W1_0, W2_0, W1_1, W2_1):
        import jax, jax.numpy as jnp
        import numpy as np
        N_NODES = 6250
        N_EDGES = 100000
        D = 64

        def _wgin_layer(x, src, dst, edge_weight, W1, W2):
            msg = edge_weight[:, None] * x[src]
            agg = jax.ops.segment_sum(msg, dst, num_segments=x.shape[0])
            h = jax.nn.relu(agg @ W1.T)
            return h @ W2.T
        src = edge_index[0]
        dst = edge_index[1]
        x = _wgin_layer(x, src, dst, edge_weight, W1_0, W2_0)
        x = _wgin_layer(x, src, dst, edge_weight, W1_1, W2_1)
        norm = jnp.linalg.norm(x, axis=1, keepdims=True)
        return x / jnp.maximum(norm, 1e-12)

    def _L2_gnn_ref(edge_index, x, W):
        import jax, jax.numpy as jnp
        import numpy as np
        N_NODES = 12500
        target = edge_index[1]
        messages = x[target] * W
        aggr = jax.ops.segment_sum(messages, target, num_segments=x.shape[0])
        return aggr

    def _L3_gnn_ref(x, edge_index, W1, as1, ad1, b1, W2, as2, ad2, b2, W3, as3, ad3, b3):
        import jax, jax.numpy as jnp
        import numpy as np
        H, C = (8, 8)
        NEG_SLOPE = 0.2

        def _leaky_relu(x):
            return jnp.where(x > 0, x, NEG_SLOPE * x)

        def _gat_layer(x, src, dst, W, a_src, a_dst, b):
            N = x.shape[0]
            h = (x @ W.T).reshape(N, H, C)
            alpha_s = jnp.einsum('nhc,hc->nh', h, a_src)
            alpha_d = jnp.einsum('nhc,hc->nh', h, a_dst)
            e = _leaky_relu(alpha_s[src] + alpha_d[dst])
            e_max = jax.ops.segment_max(e, dst, num_segments=N)
            e_exp = jnp.exp(e - e_max[dst])
            denom = jax.ops.segment_sum(e_exp, dst, num_segments=N)
            alpha = e_exp / denom[dst]
            msg = alpha[:, :, None] * h[src]
            out = jax.ops.segment_sum(msg, dst, num_segments=N)
            return out.reshape(N, H * C) + b
        N = x.shape[0]
        loops = jnp.arange(N, dtype=edge_index.dtype)
        src = jnp.concatenate([edge_index[0], loops])
        dst = jnp.concatenate([edge_index[1], loops])
        x = jax.nn.relu(_gat_layer(x, src, dst, W1, as1, ad1, b1))
        x = jax.nn.relu(_gat_layer(x, src, dst, W3, as3, ad3, b3))
        return _gat_layer(x, src, dst, W2, as2, ad2, b2)
    edge_index = jnp.stack([src, dst])
    x = _layernorm(x + _L0_gnn_ref(x, edge_index, edge_attr_16, L0_gnn_emb_ea, L0_gnn_Wl0, L0_gnn_bl0, L0_gnn_Wr0, L0_gnn_Wl1, L0_gnn_bl1, L0_gnn_Wr1, L0_gnn_Wl2, L0_gnn_bl2, L0_gnn_Wr2), axis=-1)
    x = _layernorm(x + _L1_gnn_ref(x, edge_index, edge_weight, L1_gnn_W1_0, L1_gnn_W2_0, L1_gnn_W1_1, L1_gnn_W2_1), axis=-1)
    x = _layernorm(x + _L2_gnn_ref(edge_index, x, edge_attr_64), axis=-1)
    x = _layernorm(x + _L3_gnn_ref(x, edge_index, L3_gnn_W1, L3_gnn_as1, L3_gnn_ad1, L3_gnn_b1, L3_gnn_W2, L3_gnn_as2, L3_gnn_ad2, L3_gnn_b2, L3_gnn_W3, L3_gnn_as3, L3_gnn_ad3, L3_gnn_b3), axis=-1)
    return x

_drawn_inputs = setup_inputs


def setup_inputs(seed=0):
    import zlib

    import numpy as np

    out = dict(_drawn_inputs(seed))
    spreads = {'L0_gnn_bl0': (0.0, 0.443),
     'L0_gnn_bl1': (0.0, 0.323),
     'L0_gnn_bl2': (0.0, 0.281),
     'L3_gnn_b1': (0.0, 0.307),
     'L3_gnn_b2': (0.0, 0.1),
     'L3_gnn_b3': (0.0, 0.1)}
    factors = {'edge_weight': 200.0,
     'L3_gnn_as1': 5.349,
     'L3_gnn_ad1': 200.0,
     'L3_gnn_as2': 200.0,
     'L3_gnn_ad2': 200.0,
     'L3_gnn_as3': 64.0,
     'L3_gnn_ad3': 200.0}
    for name, (base, spread) in spreads.items():
        noise = np.random.default_rng([zlib.crc32(name.encode()), seed]).standard_normal(out[name].shape)
        drawn = base * np.exp(spread * noise) if base else spread * noise
        out[name] = jnp.asarray(drawn.astype(out[name].dtype))
    for name, factor in factors.items():
        out[name] = (out[name] * factor).astype(out[name].dtype)
    return out
```

```python
import numpy as np
import concourse.bass as bass
from concourse import mybir
from concourse.alu_op_type import AluOpType as ALU
from contextlib import ExitStack

F32 = mybir.dt.float32
I32 = mybir.dt.int32
ACT = mybir.ActivationFunctionType
AX = mybir.AxisListType.X

N, E, D, EA, H, C = 6250, 206250, 64, 16, 8, 8
P = 128
G = 8
GE = G * P
NG = -(-E // GE)
EP = NG * GE
CH = 512
NCH = -(-(N + 64) // CH)
NP = NCH * CH
TC = CH // P
WIN = 48
SUB = P // H
NSUB = WIN // SUB
R = 3
ROW = D + H
BIG = float(2 ** 50)
EPS = 1e-5
SLOPE = 0.2
HALF = 101
assert NG == 2 * HALF and R * (NG // R) < NG and N % 2 == 0


def ds(start, size):
    return bass.ds(start, size)


def bc(ap, shape, axis):
    return ap.unsqueeze(axis).broadcast_to(shape)


class Sem:

    def __init__(self, handle):
        self.handle, self.base = handle, 0

    def at(self, count):
        return self.base + count

    def done(self, total):
        self.base += total


def due(count):
    return not isinstance(count, int) or count > 0


class Chain:

    def __init__(self, engine, sem):
        self.engine, self.sem, self.n, self.offset, self.per = engine, sem, 0, 0, 0

    def __call__(self, ins):
        self.n += 1
        ins.then_inc(self.sem.handle, 1)
        self.engine.wait_ge(self.sem.handle, self.sem.at(self.offset + self.n))

    def mark(self, ins):
        self.n += 1
        ins.then_inc(self.sem.handle, 1)

    def join(self):
        self.engine.wait_ge(self.sem.handle, self.sem.at(self.offset + self.n))

    def close(self):
        n, self.n = self.n, 0
        return n


def build(nc, A, out):
    ctx = ExitStack()
    with ctx:
        def sb(name, shape, dt=F32):
            return ctx.enter_context(nc.sbuf_tensor(name, shape, dt))

        def sem(name):
            return Sem(ctx.enter_context(nc.semaphore(name)))

        def dram(name, shape):
            return nc.dram_tensor(name, shape, F32, kind="Internal").ap()

        node_table = dram("node_table", (NP, D))
        gat_table = dram("gat_table", (NP, ROW))

        accT = sb("accT", [P, NP])
        auxT = sb("auxT", [P, NP])
        xT = sb("xT", [P, NP])
        X = sb("X", [P, NP // P, D])
        drel = sb("drel", [P, NG, G])
        wgt = sb("wgt", [P, NG, G])
        first = sb("first", [P, NG])
        first_i = sb("first_i", [1, NG], I32)
        span_i = sb("span_i", [1, NG], I32)
        widest = sb("widest", [1, 1])
        widest_i = sb("widest_i", [1, 1], I32)
        shift = sb("shift", [P, 1])
        base_col = sb("base_col", [P, 1])
        far_rel = sb("far_rel", [P, G])
        ident = sb("ident", [P, P])
        iota = sb("iota", [P, WIN])
        part = sb("part", [P, 1])
        subnode = sb("subnode", [P, NSUB])
        pick = sb("pick", [P, SUB])
        heads = sb("heads", [P, H])
        spread = sb("spread", [H, P])
        widen = sb("widen", [H, ROW])
        denom = sb("denom", [ROW, D])
        blk = sb("blk", [D, H])
        emb = sb("emb", [EA, D])
        names64 = ["Wl0", "Wr0", "Wl1", "Wr1", "Wl2", "Wr2", "W10", "W20", "W11", "W21", "G1", "G3", "G2"]
        wm = {n: sb(f"w_{n}", [D, D]) for n in names64}
        colnames = ["bl0", "bl1", "bl2", "gb1", "gb3", "gb2", "as1", "ad1", "as3", "ad3", "as2", "ad2"]
        cols = sb("cols", [D, len(colnames)])
        col = {n: cols[:, i:i + 1] for i, n in enumerate(colnames)}
        rowsel = {k: sb(f"rowsel{k}", [D, ROW]) for k in "132"}
        adsel = {k: sb(f"adsel{k}", [D, H]) for k in "132"}
        zeros = sb("zeros", [P, CH])
        ones = sb("ones", [H, CH])
        idx = [sb(f"idx{i}", [P, G], I32) for i in range(R)]
        rows = [sb(f"rows{i}", [P, G, ROW]) for i in range(R)]
        bufA = [sb(f"bufA{i}", [P, GE]) for i in range(R)]
        bufB = [sb(f"bufB{i}", [P, GE]) for i in range(R)]
        sel = [sb(f"sel{i}", [P, G, WIN]) for i in range(R)]
        msg = [sb(f"msg{i}", [P, G, ROW]) for i in range(R)]
        far = [sb(f"far{i}", [P, GE]) for i in range(R)]
        score8 = sb("score8", [H, GE])
        subcol = sb("subcol", [P, NSUB])
        stcol = sb("stcol", [P, 1])
        submax2 = sb("submax2", [P, NSUB, 2])
        submax = sb("submax", [P, NSUB])
        subpick = sb("subpick", [P, NSUB, SUB])
        U = sb("U", [H, 2, WIN])
        V = sb("V", [H, 2, WIN])
        dif = sb("dif", [H, WIN])
        adw = sb("adw", [H, WIN])
        res = sb("res", [H, WIN])
        avm = sb("avm", [WIN, 2 * H])
        z = sb("z", [P, G, H])
        abuf = sb("abuf", [P, CH])
        hbuf = sb("hbuf", [D, CH])
        xbuf = sb("xbuf", [D, CH])
        tbuf = sb("tbuf", [P, TC, D])
        gbuf = sb("gbuf", [P, TC, ROW])
        ybuf = sb("ybuf", [P, TC, D])
        qbuf = sb("qbuf", [P, TC, D])
        st = sb("st", [P, 4, TC])

        bank = [ctx.enter_context(nc.psum_tensor(f"bank{i}", [P, 512], F32)) for i in range(8)]

        s_load = sem("inputs_loaded")
        s_ve = sem("vector_chain")
        s_ac = sem("scalar_done")
        s_pe = sem("tensor_done")
        s_po = sem("pool_done")
        s_tab = sem("table_written")
        s_out = sem("output_written")
        s_passed = sem("waits_passed")
        s_idx = [sem(f"idx_loaded{i}") for i in range(R)]
        s_bA = [sem(f"bufA_loaded{i}") for i in range(R)]
        s_bB = [sem(f"bufB_loaded{i}") for i in range(R)]
        names = ["rows_free", "ea_ready", "sum_ready", "aux_ready", "sel_ready", "pre_ready", "msg_ready", "acc_done",
                 "auxacc_done", "scoresT_ready", "scores8_ready", "scores_ready", "cols_ready", "far_ready", "max_done",
                 "pick_ready", "winmax_ready", "shift_ready", "colsT_ready", "avm_ready", "res_ready", "wide_ready",
                 "edge_ready", "z_done", "p_ready", "selT_ready",
                 "once", "prod_ready", "mean_ready", "cleared", "nodes_ready", "tile_ready", "x_ready", "act_ready", "kept",
                 "root_asked", "root_done", "h_ready", "hprod_ready", "scored", "gtile_ready", "back_ready"]
        q = {n: sem(n) for n in names}

        loads = [(ident[:], A["c_ident"]), (iota[:], A["c_iota"]), (part[:], A["c_part"]), (subnode[:], A["c_subnode"]),
                 (pick[:], A["c_pick"]), (heads[:], A["c_heads"]), (spread[:], A["c_spread"]), (widen[:], A["c_widen"]),
                 (denom[:], A["c_denom"]), (blk[:], A["c_blk"]), (emb[:], A["emb"]), (wgt[:], A["wgt"]),
                 (X[:], A["x"].rearrange("(t p) d -> p t d", p=P)),
                 (cols[:], A["cols"])]
        loads += [(wm[n][:], A[n]) for n in names64]
        group_dst = accT[0:HALF, 0:2 * GE].bitcast(I32)
        dst_i = auxT[:, 0:NG * G].bitcast(I32)
        with nc.Block() as block:
            @block.sync
            def _(sp):
                sp.dma_start(group_dst.rearrange("p (h e) -> p h e", h=2),
                             A["dst_rows"].rearrange("(h p) e -> p h e", p=HALF)).then_inc(s_load.handle, 16)
                sp.dma_start(dst_i, A["dst"]).then_inc(s_load.handle, 16)
                for o, i in loads:
                    sp.dma_start(o, i).then_inc(s_load.handle, 16)

            @block.vector
            def _(ve):
                link = Chain(ve, s_ve)
                ve.wait_ge(s_load.handle, s_load.at(16 * (len(loads) + 2)))
                ends = st[0:HALF, 0:2, 0:2]
                for h in range(2):
                    src = group_dst[:, h * GE:(h + 1) * GE]
                    link.mark(nc.vector.tensor_reduce(ends[:, 0, h:h + 1], src, AX, ALU.min))
                    link.mark(nc.vector.tensor_reduce(ends[:, 1, h:h + 1], src, AX, ALU.max))
                link.join()
                for e in range(2):
                    for h in range(2):
                        link.mark(nc.vector.tensor_scalar(abuf[0:HALF, (2 * e + h) * HALF:(2 * e + h + 1) * HALF],
                                                          ident[0:HALF, 0:HALF], ends[:, e, h:h + 1], None, ALU.mult))
                link.mark(nc.vector.memset(ybuf[:], 1.0))
                link.mark(nc.vector.memset(zeros[:], 0.0))
                link.mark(nc.vector.memset(ones[:], 1.0))
                for i in range(R):
                    link.mark(nc.vector.memset(bufA[i][:], 1.0))
                for k in "132":
                    link.mark(nc.vector.tensor_copy(rowsel[k][:, 0:D], ident[0:D, 0:D]))
                    link.mark(nc.vector.tensor_scalar(rowsel[k][:, D:ROW], blk[:], col["as" + k], None, ALU.mult))
                    link.mark(nc.vector.tensor_scalar(adsel[k][:], blk[:], col["ad" + k], None, ALU.mult))
                link.join()
                ve.wait_ge(s_pe.handle, s_pe.at(1))
                link(nc.vector.tensor_copy(first[:], bank[0][:, 0:NG]))
                link(nc.vector.tensor_copy(first_i[:], bank[0][0:1, 0:NG]))
                link(nc.vector.tensor_copy(span_i[:], bank[0][0:1, NG:2 * NG]))
                link(nc.vector.tensor_tensor(span_i[:], span_i[:], first_i[:], ALU.subtract))
                link(nc.vector.tensor_reduce(widest[:], span_i[:], AX, ALU.max))
                link(nc.vector.tensor_copy(widest_i[:], widest[:]))
                link(nc.vector.tensor_copy(drel[:].rearrange("p g j -> p (g j)"), dst_i))
                link(nc.vector.tensor_tensor(drel[:], drel[:], bc(first[:], [P, NG, G], 2), ALU.subtract))
                link(nc.vector.memset(accT[:], 0.0))
                link(nc.vector.memset(auxT[:], 0.0))
                if due(1 + NP // P):
                    ve.wait_ge(s_pe.handle, s_pe.at(1 + NP // P))
                s_ve.total = link.close()

            @block.tensor
            def _(pe):
                pe.wait_ge(s_ve.handle, s_ve.at(4 + 4 + 3 + R + 9))
                all_ones = ybuf[0:HALF, 0:2, :].rearrange("p a b -> p (a b)")
                nc.tensor.matmul(bank[0][:, 0:4 * HALF], all_ones, abuf[0:HALF, 0:4 * HALF],
                                 start=True, stop=True).then_inc(s_pe.handle, 1)
                for t in range(NP // P):
                    b = 1 + t % 2
                    if due(t - 1):
                        pe.wait_ge(s_ac.handle, s_ac.at(t - 1))
                    nc.tensor.matmul(bank[b][0:D, 0:P], X[:, t, :], ident[:], start=True, stop=True).then_inc(s_pe.handle, 1)

            @block.scalar
            def _(ac):
                for t in range(NP // P):
                    ac.wait_ge(s_pe.handle, s_pe.at(t + 2))
                    nc.scalar.activation(xT[0:D, t * P:(t + 1) * P], bank[1 + t % 2][0:D, 0:P],
                                         ACT.Copy).then_inc(s_ac.handle, 1)
        s_ve.done(s_ve.total)
        s_pe.done(1 + NP // P)
        s_ac.done(NP // P)

        def turns(body):
            for g in range(R):
                body(g, g, 0)

            def rest(fori):
                with fori(1, NG // R) as it:
                    for s in range(R):
                        body(it * R + s, s, it)
                for g in range(R * (NG // R), NG):
                    body(g, g % R, g // R)
            return rest

        def slot_total(s):
            return NG // R + (s < NG % R)

        token_vector_vector = sem("token_vector_to_vector")
        token_vector_scalar = sem("token_vector_to_scalar")
        token_scalar_vector = sem("token_scalar_to_vector")
        token_vector_tensor = sem("token_vector_to_tensor")
        token_tensor_vector = sem("token_tensor_to_vector")
        token_tensor_scalar = sem("token_tensor_to_scalar")
        token_scalar_tensor = sem("token_scalar_to_tensor")

        def settle(ve, ins):
            ins.then_inc(token_vector_vector.handle, 1)
            ve.wait_ge(token_vector_vector.handle, 1)
            ve.sem_clear(token_vector_vector.handle)

        def further(engine, group, window=None, closing=None):
            widest_reg = engine.value_load(widest_i[0:1, 0:1], min_val=0, max_val=N)
            with engine.If(widest_reg >= WIN):
                with engine.Fori(0, NG) as g:
                    group(g)
                    if window is not None:
                        span = engine.value_load(span_i[0:1, ds(g, 1)], min_val=0, max_val=N)
                        start = engine.value_load(first_i[0:1, ds(g, 1)], min_val=0, max_val=N)
                        with engine.If(span >= WIN):
                            with engine.Fori(1, span // WIN + 1) as k:
                                window(g, k, start + k * WIN)
                    if closing is not None:
                        closing(g)
                engine.nop()

        def next_window(ve, g):
            settle(ve, nc.vector.tensor_scalar(shift[:], shift[:], float(WIN), None, ALU.add))
            settle(ve, nc.vector.tensor_scalar(far_rel[:], drel[:, ds(g, 1), :].rearrange("p o j -> p (o j)"), shift[:],
                                               None, ALU.subtract))
            return nc.vector.tensor_tensor(sel[0][:], bc(iota[:], [P, G, WIN], 1), bc(far_rel[:], [P, G, WIN], 2),
                                           ALU.is_equal)

        def sum_further(name, table, attr, aux):
            f_load, f_rows, f_ea, f_done = (sem(f"{name}_further_{n}") for n in ["loaded", "rows_loaded", "ea_ready", "group_done"])
            n_load = 1 + attr + aux
            with nc.Block() as block:
                @block.sync
                def _(sp):
                    def group(g):
                        sp.wait_ge(f_done.handle, g + 1)
                        sp.dma_start(idx[0][:], A["src"][ds(g, 1), :, :].rearrange("o p j -> (o p) j")
                                     ).then_inc(f_load.handle, 16)
                        if attr:
                            sp.dma_start(bufB[0][0:EA, :], A["attr16"][ds(g, 1), :, :].rearrange("o k e -> (o k) e")
                                         ).then_inc(f_load.handle, 16)
                        if aux:
                            sp.dma_start(bufA[0][:].rearrange("p (j d) -> p j d", d=P)[:, :, D:P],
                                         A["attr64"][ds(g, 1), :, :].rearrange("o p (j d) -> (o p) j d", d=D)
                                         ).then_inc(f_load.handle, 16)
                    further(sp, group)

                @block.gpsimd
                def _(po):
                    def group(g):
                        po.wait_ge(f_load.handle, f_load.at((g + 1) * 16 * n_load))
                        po.sem_inc(s_passed.handle, 1)
                        for j in range(G):
                            nc.gpsimd.indirect_dma_start(rows[0][:, j, 0:D], None, table,
                                                         bass.IndirectOffsetOnAxis(idx[0][:, j:j + 1], 0)
                                                         ).then_inc(f_rows.handle, 16)
                    further(po, group)

                @block.tensor
                def _(pe):
                    def group(g):
                        pe.wait_ge(f_load.handle, (g + 1) * 16 * n_load)
                        if attr:
                            for j in range(G):
                                last = nc.tensor.matmul(bank[0][:, j * D:(j + 1) * D], bufB[0][0:EA, j * P:(j + 1) * P],
                                                        emb[:], start=True, stop=True)
                            last.then_inc(f_ea.handle, 1)

                    def window(g, k, start):
                        pe.wait_ge(token_vector_tensor.handle, 1)
                        pe.sem_clear(token_vector_tensor.handle)
                        if aux:
                            for j in range(G):
                                nc.tensor.matmul(bank[6][:, 0:WIN], bufA[0][:, j * P:(j + 1) * P], sel[0][:, j, :],
                                                 start=j == 0, stop=j == G - 1)
                        for j in range(G):
                            last = nc.tensor.matmul(bank[3][0:D, 0:WIN], msg[0][:, j, 0:D], sel[0][:, j, :],
                                                    start=j == 0, stop=j == G - 1)
                        last.then_inc(token_tensor_vector.handle, 1)
                    further(pe, group, window)

                @block.vector
                def _(ve):
                    nc.vector.memset(shift[:], 0.0).then_inc(f_done.handle, 1)

                    def group(g):
                        ve.wait_ge(f_rows.handle, (g + 1) * 16 * G)
                        if attr:
                            ve.wait_ge(f_ea.handle, g + 1)
                            summed = far[0][:, 0:G * D].rearrange("p (j d) -> p j d", d=D)
                            settle(ve, nc.vector.tensor_tensor(summed, rows[0][:, :, 0:D],
                                                               bank[0][:].rearrange("p (j d) -> p j d", d=D), ALU.add))
                            settle(ve, nc.vector.tensor_scalar(msg[0][:, :, 0:D], summed, 0.0, None, ALU.max))
                        else:
                            settle(ve, nc.vector.tensor_tensor(msg[0][:, :, 0:D], rows[0][:, :, 0:D],
                                                               bc(wgt[:, ds(g, 1), :].rearrange("p o j -> p (o j)"), [P, G, D], 2),
                                                               ALU.mult))
                        settle(ve, nc.vector.memset(shift[:], 0.0))

                    def window(g, k, start):
                        next_window(ve, g).then_inc(token_vector_tensor.handle, 1)
                        ve.wait_ge(token_tensor_vector.handle, 1)
                        ve.sem_clear(token_tensor_vector.handle)
                        start = nc.s_assert_within(start, 0, N, skip_runtime_bounds_check_because="a window starts at or below the last destination")
                        w = accT[0:D, ds(start, WIN)]
                        settle(ve, nc.vector.tensor_tensor(w, w, bank[3][0:D, 0:WIN], ALU.add))
                        if aux:
                            w = auxT[:, ds(start, WIN)]
                            settle(ve, nc.vector.tensor_tensor(w, w, bank[6][:, 0:WIN], ALU.add))

                    def closing(g):
                        nc.vector.memset(base_col[:], 0.0).then_inc(f_done.handle, 1)
                    further(ve, group, window, closing)

        def gat_further(name):
            f_load, f_rows, f_scores, f_done, f_8 = (sem(f"{name}_further_{n}") for n in
                                                     ["loaded", "rows_loaded", "scores_ready", "group_done", "scores8_ready"])
            with nc.Block() as block:
                @block.sync
                def _(sp):
                    def group(g):
                        sp.wait_ge(f_done.handle, g + 1)
                        sp.dma_start(idx[0][:], A["src"][ds(g, 1), :, :].rearrange("o p j -> (o p) j")
                                     ).then_inc(f_load.handle, 16)
                        sp.dma_start(bufA[0][:].bitcast(I32), A["dst_rows"][ds(g, 1), :].broadcast_to([P, GE])
                                     ).then_inc(f_load.handle, 16)
                    further(sp, group)

                @block.gpsimd
                def _(po):
                    def group(g):
                        po.wait_ge(f_load.handle, f_load.at((g + 1) * 32))
                        po.sem_inc(s_passed.handle, 1)
                        for j in range(G):
                            nc.gpsimd.indirect_dma_start(rows[0][:, j, :], None, gat_table,
                                                         bass.IndirectOffsetOnAxis(idx[0][:, j:j + 1], 0)
                                                         ).then_inc(f_rows.handle, 16)
                    further(po, group)

                @block.tensor
                def _(pe):
                    def group(g):
                        pe.wait_ge(f_rows.handle, (g + 1) * 16 * G)
                        for j in range(G):
                            last = nc.tensor.matmul(bank[j // 4][0:H, (j % 4) * P:(j % 4 + 1) * P], rows[0][:, j, D:ROW],
                                                    ident[:], start=True, stop=True)
                        last.then_inc(f_scores.handle, 1)
                        pe.wait_ge(f_8.handle, g + 1)
                        for h in range(2):
                            last = nc.tensor.matmul(bank[2 + h][:], spread[:], score8[:, h * 512:(h + 1) * 512],
                                                    start=True, stop=True)
                        last.then_inc(f_scores.handle, 1)

                    def window(g, k, start):
                        pe.wait_ge(token_vector_tensor.handle, 1)
                        pe.sem_clear(token_vector_tensor.handle)
                        nc.tensor.matmul(bank[6][0:H, 0:WIN], heads[:], subpick[:].rearrange("p a b -> p (a b)"),
                                              start=True, stop=True).then_inc(token_tensor_vector.handle, 1)
                        pe.wait_ge(token_vector_tensor.handle, 1)
                        pe.sem_clear(token_vector_tensor.handle)
                        nc.tensor.matmul(bank[6][0:WIN, 64:64 + H], adw[:], ident[0:H, 0:H], start=True, stop=True)
                        nc.tensor.matmul(bank[6][0:WIN, 64 + H:64 + 2 * H], V[:, 1, :], ident[0:H, 0:H],
                                              start=True, stop=True).then_inc(token_tensor_scalar.handle, 1)
                        pe.wait_ge(token_scalar_tensor.handle, 1)
                        pe.sem_clear(token_scalar_tensor.handle)
                        nc.tensor.matmul(bank[5][0:ROW, 64:64 + WIN], widen[:], res[:], start=True, stop=True)
                        for j in range(G):
                            last = nc.tensor.matmul(bank[4][:, j * 2 * H:(j + 1) * 2 * H], bufB[0][0:WIN, j * P:(j + 1) * P],
                                                    avm[:], start=True, stop=True)
                        last.then_inc(token_tensor_vector.handle, 1)
                        pe.wait_ge(token_vector_tensor.handle, 1)
                        pe.sem_clear(token_vector_tensor.handle)
                        for j in range(G):
                            last = nc.tensor.matmul(bank[5][0:ROW, 0:WIN], msg[0][:, j, :], sel[0][:, j, :],
                                                    start=j == 0, stop=j == G - 1)
                        last.then_inc(token_tensor_vector.handle, 1)
                    further(pe, group, window)

                @block.scalar
                def _(ac):
                    def group(g):
                        ac.wait_ge(f_scores.handle, 2 * g + 1)
                        for h in range(2):
                            last = nc.scalar.activation(score8[:, h * 512:(h + 1) * 512], bank[h][0:H, :], ACT.Copy)
                        last.then_inc(f_8.handle, 1)

                    def window(g, k, start):
                        ac.wait_ge(token_vector_scalar.handle, 1)
                        ac.sem_clear(token_vector_scalar.handle)
                        for n in range(NSUB):
                            last = nc.scalar.activation(far[n][:], bufA[0][:].bitcast(I32), ACT.Square,
                                                        bias=subcol[:, n:n + 1], scale=BIG)
                        last.then_inc(token_scalar_vector.handle, 1)
                        ac.wait_ge(token_tensor_scalar.handle, 1)
                        ac.sem_clear(token_tensor_scalar.handle)
                        nc.scalar.activation(res[:], dif[:], ACT.Exp)
                        nc.scalar.activation(avm[:], bank[6][0:WIN, 64:64 + 2 * H], ACT.Copy).then_inc(token_scalar_tensor.handle, 1)
                        ac.wait_ge(token_vector_scalar.handle, 1)
                        ac.sem_clear(token_vector_scalar.handle)
                        nc.scalar.activation(msg[0][:, :, D:ROW], z[:], ACT.Exp).then_inc(token_scalar_vector.handle, 1)
                    further(ac, group, window)

                @block.vector
                def _(ve):
                    nc.vector.memset(shift[:], 0.0).then_inc(f_done.handle, 1)

                    def group(g):
                        ve.wait_ge(f_load.handle, (g + 1) * 32)
                        ve.wait_ge(f_scores.handle, 2 * g + 2)
                        settle(ve, nc.vector.memset(shift[:], 0.0))

                    def window(g, k, start):
                        settle(ve, next_window(ve, g))
                        settle(ve, nc.vector.tensor_tensor(base_col[:], first[:, ds(g, 1)], shift[:], ALU.add))
                        settle(ve, nc.vector.tensor_tensor(stcol[:], part[:], base_col[:], ALU.add))
                        settle(ve, nc.vector.tensor_scalar(bufB[0][0:WIN, :], bufA[0][0:WIN, :].bitcast(I32), stcol[0:WIN, :],
                                                           None, ALU.is_equal))
                        nc.vector.tensor_scalar(subcol[:], subnode[:], base_col[:], -BIG, ALU.add, ALU.mult).then_inc(token_vector_scalar.handle, 1)
                        ve.wait_ge(token_scalar_vector.handle, 1)
                        ve.sem_clear(token_scalar_vector.handle)
                        for n in range(NSUB):
                            for h in range(2):
                                last = nc.vector.tensor_tensor_reduce(
                                    out=far[n][:, h * 512:(h + 1) * 512], in0=bank[2 + h][:],
                                    in1=far[n][:, h * 512:(h + 1) * 512], scale=1.0, scalar=-3.0e38, op0=ALU.subtract,
                                    op1=ALU.max, accum_out=submax2[:, n, h:h + 1])
                        settle(ve, last)
                        settle(ve, nc.vector.tensor_reduce(submax[:], submax2[:], AX, ALU.max))
                        nc.vector.tensor_tensor(subpick[:], bc(submax[:], [P, NSUB, SUB], 2),
                                                     bc(pick[:], [P, NSUB, SUB], 1), ALU.mult).then_inc(token_vector_tensor.handle, 1)
                        ve.wait_ge(token_tensor_vector.handle, 1)
                        ve.sem_clear(token_tensor_vector.handle)
                        start = nc.s_assert_within(start, 0, N, skip_runtime_bounds_check_because="a window starts at or below the last destination")
                        m = xT[0:H, ds(start, WIN)]
                        a = auxT[0:H, ds(start, WIN)]
                        nc.vector.tensor_copy(adw[:], a)
                        settle(ve, nc.vector.tensor_tensor(U[:, 0, :], m, a, ALU.add))
                        settle(ve, nc.vector.tensor_tensor(m, m, bank[6][0:H, 0:WIN], ALU.max))
                        settle(ve, nc.vector.tensor_tensor(U[:, 1, :], m, a, ALU.add))
                        settle(ve, nc.vector.scalar_tensor_tensor(V[:], U[:], SLOPE, U[:], ALU.mult, ALU.max))
                        nc.vector.tensor_tensor(dif[:], V[:, 0, :], V[:, 1, :], ALU.subtract).then_inc(token_vector_tensor.handle, 1)
                        ve.wait_ge(token_tensor_vector.handle, 1)
                        ve.sem_clear(token_tensor_vector.handle)
                        ed = bank[4][:, 0:G * 2 * H].rearrange("p (j v) -> p j v", v=2 * H)
                        settle(ve, nc.vector.tensor_tensor(z[:], rows[0][:, :, D:ROW], ed[:, :, 0:H], ALU.add))
                        settle(ve, nc.vector.scalar_tensor_tensor(z[:], z[:], SLOPE, z[:], ALU.mult, ALU.max))
                        settle(ve, nc.vector.tensor_tensor(z[:], z[:], ed[:, :, H:2 * H], ALU.subtract))
                        nc.vector.tensor_scalar(z[:], z[:], 0.0, None, ALU.min).then_inc(token_vector_scalar.handle, 1)
                        ve.wait_ge(token_scalar_vector.handle, 1)
                        ve.sem_clear(token_scalar_vector.handle)
                        nc.vector.tensor_tensor(msg[0][:, :, 0:D].rearrange("p j (h c) -> p j h c", c=C),
                                                     rows[0][:, :, 0:D].rearrange("p j (h c) -> p j h c", c=C),
                                                     bc(msg[0][:, :, D:ROW], [P, G, H, C], 3), ALU.mult).then_inc(token_vector_tensor.handle, 1)
                        ve.wait_ge(token_tensor_vector.handle, 1)
                        ve.sem_clear(token_tensor_vector.handle)
                        w = accT[0:ROW, ds(start, WIN)]
                        settle(ve, nc.vector.tensor_tensor(w, w, bank[5][0:ROW, 64:64 + WIN], ALU.mult))
                        settle(ve, nc.vector.tensor_tensor(w, w, bank[5][0:ROW, 0:WIN], ALU.add))

                    def closing(g):
                        nc.vector.memset(base_col[:], 0.0).then_inc(f_done.handle, 1)
                    further(ve, group, window, closing)

        def sum_pass(name, table, attr=False, aux=False):
            s_rows = [sem(f"{name}_rows_loaded{i}") for i in range(R)]
            with nc.Block() as block:
                @block.sync
                def _(sp):
                    def body(g, s, it):
                        if due(it * 16 * G):
                            sp.wait_ge(s_rows[s].handle, s_rows[s].at(it * 16 * G))
                        sp.dma_start(idx[s][:], A["src"][ds(g, 1), :, :].rearrange("o p j -> (o p) j")
                                     ).then_inc(s_idx[s].handle, 16)
                        if attr:
                            if due(g - R + 1):
                                sp.wait_ge(q["ea_ready"].handle, q["ea_ready"].at(g - R + 1))
                            sp.dma_start(bufB[s][0:EA, :], A["attr16"][ds(g, 1), :, :].rearrange("o k e -> (o k) e")
                                         ).then_inc(s_bB[s].handle, 16)
                        if aux:
                            if due(g - R + 1):
                                sp.wait_ge(q["aux_ready"].handle, q["aux_ready"].at(g - R + 1))
                            sp.dma_start(bufA[s][:].rearrange("p (j d) -> p j d", d=P)[:, :, D:P],
                                         A["attr64"][ds(g, 1), :, :].rearrange("o p (j d) -> (o p) j d", d=D)
                                         ).then_inc(s_bA[s].handle, 16)
                    turns(body)(sp.Fori)

                @block.gpsimd
                def _(po):
                    def body(g, s, it):
                        po.wait_ge(s_idx[s].handle, s_idx[s].at(it * 16 + 16))
                        if due(g - R + 1):
                            po.wait_ge(q["rows_free" if attr else "msg_ready"].handle, q["rows_free" if attr else "msg_ready"].at(g - R + 1))
                        po.sem_inc(s_passed.handle, 1)
                        for j in range(G):
                            nc.gpsimd.indirect_dma_start(rows[s][:, j, 0:D], None, table,
                                                         bass.IndirectOffsetOnAxis(idx[s][:, j:j + 1], 0)
                                                         ).then_inc(s_rows[s].handle, 16)
                    turns(body)(po.Fori)

                @block.tensor
                def _(pe):
                    def body(g, s, it):
                        if attr:
                            pe.wait_ge(s_bB[s].handle, s_bB[s].at(it * 16 + 16))
                            if due(g - R + 1):
                                pe.wait_ge(q["rows_free"].handle, q["rows_free"].at(g - R + 1))
                            for j in range(G):
                                last = nc.tensor.matmul(bank[s][:, j * D:(j + 1) * D],
                                                        bufB[s][0:EA, j * P:(j + 1) * P], emb[:], start=True, stop=True)
                            last.then_inc(q["ea_ready"].handle, 1)
                        pe.wait_ge(q["sel_ready"].handle, q["sel_ready"].at(g + 1))
                        if aux:
                            pe.wait_ge(s_bA[s].handle, s_bA[s].at(it * 16 + 16))
                            if due(g):
                                pe.wait_ge(q["auxacc_done"].handle, q["auxacc_done"].at(g))
                            for j in range(G):
                                last = nc.tensor.matmul(bank[6][:, 0:WIN], bufA[s][:, j * P:(j + 1) * P], sel[s][:, j, :],
                                                        start=j == 0, stop=j == G - 1)
                            last.then_inc(q["aux_ready"].handle, 1)
                        pe.wait_ge(q["msg_ready"].handle, q["msg_ready"].at(g + 1))
                        if due(g - R + 1):
                            pe.wait_ge(q["acc_done"].handle, q["acc_done"].at(g - R + 1))
                        for j in range(G):
                            last = nc.tensor.matmul(bank[3 + s][0:D, 0:WIN], msg[s][:, j, 0:D], sel[s][:, j, :],
                                                    start=j == 0, stop=j == G - 1)
                        last.then_inc(q["sum_ready"].handle, 1)
                    turns(body)(pe.Fori)

                @block.vector
                def _(ve):
                    def add_sums(g, s):
                        base = ve.value_load(first_i[0:1, ds(g, 1)], min_val=0, max_val=N)
                        w = accT[0:D, ds(base, WIN)]
                        ve.wait_ge(q["sum_ready"].handle, q["sum_ready"].at(g + 1))
                        if due(g):
                            ve.wait_ge(q["acc_done"].handle, q["acc_done"].at(g))
                        nc.vector.tensor_tensor(w, w, bank[3 + s][0:D, 0:WIN], ALU.add).then_inc(q["acc_done"].handle, 1)
                        if aux:
                            if due(g):
                                ve.wait_ge(q["auxacc_done"].handle, q["auxacc_done"].at(g))
                            w = auxT[:, ds(base, WIN)]
                            nc.vector.tensor_tensor(w, w, bank[6][:, 0:WIN], ALU.add).then_inc(q["auxacc_done"].handle, 1)

                    def body(g, s, it):
                        if due(g - R + 1):
                            ve.wait_ge(q["sum_ready"].handle, q["sum_ready"].at(g - R + 1))
                        nc.vector.tensor_tensor(sel[s][:], bc(iota[:], [P, G, WIN], 1), bc(drel[:, ds(g, 1), :].rearrange("p o j -> p (o j)"), [P, G, WIN], 2),
                                                ALU.is_equal).then_inc(q["sel_ready"].handle, 1)
                        if not (isinstance(g, int) and g == 0):
                            add_sums(g - 1, (s - 1) % R)
                        ve.wait_ge(s_rows[s].handle, s_rows[s].at((it + 1) * 16 * G))
                        if attr:
                            ve.wait_ge(q["ea_ready"].handle, q["ea_ready"].at(g + 1))
                            if due(g - R + 1):
                                ve.wait_ge(q["msg_ready"].handle, q["msg_ready"].at(g - R + 1))
                            nc.vector.tensor_tensor(far[s][:, 0:G * D].rearrange("p (j d) -> p j d", d=D), rows[s][:, :, 0:D],
                                                    bank[s][:].rearrange("p (j d) -> p j d", d=D), ALU.add
                                                    ).then_inc(q["rows_free"].handle, 1)
                        else:
                            nc.vector.tensor_tensor(msg[s][:, :, 0:D], rows[s][:, :, 0:D],
                                                    bc(wgt[:, ds(g, 1), :].rearrange("p o j -> p (o j)"), [P, G, D], 2), ALU.mult
                                                    ).then_inc(q["msg_ready"].handle, 1)
                    turns(body)(ve.Fori)
                    add_sums(NG - 1, (NG - 1) % R)

                if attr:
                    @block.scalar
                    def _(ac):
                        def body(g, s, it):
                            ac.wait_ge(q["rows_free"].handle, q["rows_free"].at(g + 1))
                            if due(g - R + 1):
                                ac.wait_ge(q["sum_ready"].handle, q["sum_ready"].at(g - R + 1))
                            nc.scalar.activation(msg[s][:, :, 0:D], far[s][:, 0:G * D].rearrange("p (j d) -> p j d", d=D),
                                                 ACT.Relu).then_inc(q["msg_ready"].handle, 1)
                        turns(body)(ac.Fori)
            for s in range(R):
                s_idx[s].done(16 * slot_total(s))
                if attr:
                    s_bB[s].done(16 * slot_total(s))
                if aux:
                    s_bA[s].done(16 * slot_total(s))
            for n in ["sel_ready", "msg_ready", "acc_done", "sum_ready"] + ["ea_ready", "rows_free"] * attr + ["aux_ready", "auxacc_done"] * aux:
                q[n].done(NG)
            sum_further(name, table, attr, aux)

        def chunks(fori, body, link=None):
            body(0)
            if link is not None:
                link.per = link.close()
            with fori(1, NCH) as c:
                if link is not None:
                    link.offset = c * link.per
                body(c)
            if link is not None:
                assert link.close() == link.per
                link.sem.total = link.per * NCH

        LO = slice(0, D)

        def chunk(table, part_rows, c):
            return table[part_rows, ds(c * CH, CH)]

        def tiles(c):
            return X[:, ds(c * TC, TC), :]

        def table_rows(table, c):
            return table[ds(c * CH, CH), :].rearrange("(t p) d -> p t d", p=P)

        def by_tile(b, width=D):
            return b[:, 0:TC * width].rearrange("p (t d) -> p t d", d=width)

        def to_nodes(b, src, rhs, width):
            for t in range(TC):
                last = nc.tensor.matmul(b[:, t * width:(t + 1) * width], src[:, t * P:(t + 1) * P], rhs,
                                        start=True, stop=True)
            return last

        def layer_norm(ve, link, y, o, n):
            link(nc.vector.tensor_reduce(st[:, 0, :], y[:], AX, ALU.add))
            link(nc.vector.tensor_scalar(st[:, 0, :], st[:, 0, :], 1.0 / D, None, ALU.mult))
            link(nc.vector.tensor_tensor(y[:], y[:], bc(st[:, 0, :], [P, TC, D], 2), ALU.subtract))
            link(nc.vector.tensor_tensor(qbuf[:], y[:], y[:], ALU.mult))
            link(nc.vector.tensor_reduce(st[:, 1, :], qbuf[:], AX, ALU.add))
            nc.vector.tensor_scalar(st[:, 1, :], st[:, 1, :], 1.0 / D, EPS, ALU.mult, ALU.add
                                    ).then_inc(q["root_asked"].handle, 1)
            ve.wait_ge(q["root_done"].handle, q["root_done"].at(n))
            link(nc.vector.reciprocal(st[:, 3, :], st[:, 2, :]))
            return nc.vector.tensor_tensor(o[:], y[:], bc(st[:, 3, :], [P, TC, D], 2), ALU.mult)

        def root(ac, n):
            ac.wait_ge(q["root_asked"].handle, q["root_asked"].at(n))
            nc.scalar.activation(st[:, 2, :], st[:, 1, :], ACT.Sqrt).then_inc(q["root_done"].handle, 1)

        def sage_dense(i):
            last_one = i == 2
            with nc.Block() as block:
                @block.vector
                def _(ve):
                    link = Chain(ve, s_ve)
                    if i == 0:
                        cnt = auxT[LO, :]
                        nc.vector.tensor_scalar(cnt, cnt, 1.0, None, ALU.max).then_inc(q["once"].handle, 1)
                        ve.wait_ge(q["once"].handle, q["once"].at(1))
                        nc.vector.reciprocal(cnt, cnt).then_inc(q["once"].handle, 1)
                        ve.wait_ge(q["once"].handle, q["once"].at(2))

                    def body(c):
                        if due(c):
                            ve.wait_ge(q["prod_ready"].handle, q["prod_ready"].at(c))
                        nc.vector.tensor_tensor(abuf[LO, :], chunk(accT, LO, c), chunk(auxT, LO, c), ALU.mult
                                                ).then_inc(q["mean_ready"].handle, 1)
                        ve.wait_ge(q["mean_ready"].handle, q["mean_ready"].at(c + 1))
                        ve.sem_inc(s_passed.handle, 1)
                        nc.vector.tensor_copy(chunk(accT, LO, c), zeros[LO, :]).then_inc(q["cleared"].handle, 1)
                        ve.wait_ge(q["nodes_ready"].handle, q["nodes_ready"].at(c + 1))
                        if due(16 * c):
                            ve.wait_ge(s_tab.handle, s_tab.at(16 * c))
                        if last_one:
                            link(nc.vector.tensor_tensor(ybuf[:], by_tile(bank[1]), tiles(c), ALU.add))
                            link(layer_norm(ve, link, ybuf, tbuf, c + 1))
                            ve.sem_inc(s_passed.handle, 1)
                            nc.vector.tensor_copy(tiles(c), tbuf[:]).then_inc(q["tile_ready"].handle, 1)
                        else:
                            nc.vector.tensor_copy(tbuf[:], by_tile(bank[1])).then_inc(q["tile_ready"].handle, 1)
                    chunks(ve.Fori, body, link)

                @block.tensor
                def _(pe):
                    def body(c):
                        pe.wait_ge(q["mean_ready"].handle, q["mean_ready"].at(c + 1))
                        pe.wait_ge(q["x_ready"].handle, q["x_ready"].at(c + 1))
                        if due(c):
                            pe.wait_ge(q["act_ready"].handle, q["act_ready"].at(c))
                        pe.sem_inc(s_passed.handle, 1)
                        nc.tensor.matmul(bank[0][LO, :], wm[f"Wl{i}"][:], abuf[LO, :], start=True, stop=False)
                        nc.tensor.matmul(bank[0][LO, :], wm[f"Wr{i}"][:], xbuf[:], start=False, stop=True
                                         ).then_inc(q["prod_ready"].handle, 1)
                        pe.wait_ge(q["act_ready"].handle, q["act_ready"].at(c + 1))
                        if due(c):
                            pe.wait_ge(q["tile_ready"].handle, q["tile_ready"].at(c))
                        pe.sem_inc(s_passed.handle, 1)
                        to_nodes(bank[1], hbuf, ident[LO, LO], D).then_inc(q["nodes_ready"].handle, 1)
                    chunks(pe.Fori, body)

                @block.scalar
                def _(ac):
                    def body(c):
                        if due(c):
                            ac.wait_ge(q["prod_ready"].handle, q["prod_ready"].at(c))
                        nc.scalar.activation(xbuf[:], chunk(xT, LO, c), ACT.Copy).then_inc(q["x_ready"].handle, 1)
                        ac.wait_ge(q["prod_ready"].handle, q["prod_ready"].at(c + 1))
                        if due(c):
                            ac.wait_ge(q["nodes_ready"].handle, q["nodes_ready"].at(c))
                        nc.scalar.activation(hbuf[:], bank[0][LO, :], ACT.Identity if last_one else ACT.Relu,
                                             bias=col[f"bl{i}"]).then_inc(q["act_ready"].handle, 1)
                        if last_one:
                            root(ac, c + 1)
                        else:
                            ac.wait_ge(q["act_ready"].handle, q["act_ready"].at(c + 1))
                            ac.sem_inc(s_passed.handle, 1)
                            nc.scalar.activation(chunk(xT, LO, c), hbuf[:], ACT.Copy).then_inc(q["kept"].handle, 1)
                    chunks(ac.Fori, body)

                @block.sync
                def _(sp):
                    def body(c):
                        sp.wait_ge(q["tile_ready"].handle, q["tile_ready"].at(c + 1))
                        sp.dma_start(table_rows(node_table, c), tbuf[:]).then_inc(s_tab.handle, 16)
                    chunks(sp.Fori, body)
                    sp.wait_ge(s_tab.handle, s_tab.at(16 * NCH))
            s_ve.done(s_ve.total)
            s_tab.done(16 * NCH)
            q["once"].done(2 * (i == 0))
            for n in ["prod_ready", "mean_ready", "cleared", "nodes_ready", "tile_ready", "x_ready", "act_ready"]:
                q[n].done(NCH)
            for n in ["root_asked", "root_done"] if last_one else ["kept"]:
                q[n].done(NCH)

        def gin_dense0():
            with nc.Block() as block:
                @block.vector
                def _(ve):
                    def body(c):
                        if due(c):
                            ve.wait_ge(q["prod_ready"].handle, q["prod_ready"].at(c))
                        nc.vector.tensor_copy(abuf[LO, :], chunk(accT, LO, c)).then_inc(q["mean_ready"].handle, 1)
                        ve.wait_ge(q["mean_ready"].handle, q["mean_ready"].at(c + 1))
                        ve.sem_inc(s_passed.handle, 1)
                        nc.vector.tensor_copy(chunk(accT, LO, c), zeros[LO, :]).then_inc(q["cleared"].handle, 1)
                        ve.wait_ge(q["nodes_ready"].handle, q["nodes_ready"].at(c + 1))
                        if due(16 * c):
                            ve.wait_ge(s_tab.handle, s_tab.at(16 * c))
                        nc.vector.tensor_copy(tbuf[:], by_tile(bank[1])).then_inc(q["tile_ready"].handle, 1)
                    chunks(ve.Fori, body)

                @block.tensor
                def _(pe):
                    def body(c):
                        pe.wait_ge(q["mean_ready"].handle, q["mean_ready"].at(c + 1))
                        if due(c):
                            pe.wait_ge(q["act_ready"].handle, q["act_ready"].at(c))
                        pe.sem_inc(s_passed.handle, 1)
                        nc.tensor.matmul(bank[0][LO, :], wm["W10"][:], abuf[LO, :], start=True, stop=True
                                         ).then_inc(q["prod_ready"].handle, 1)
                        pe.wait_ge(q["act_ready"].handle, q["act_ready"].at(c + 1))
                        if due(c):
                            pe.wait_ge(q["tile_ready"].handle, q["tile_ready"].at(c))
                        to_nodes(bank[1], hbuf, wm["W20"][:], D).then_inc(q["nodes_ready"].handle, 1)
                    chunks(pe.Fori, body)

                @block.scalar
                def _(ac):
                    def body(c):
                        ac.wait_ge(q["prod_ready"].handle, q["prod_ready"].at(c + 1))
                        if due(c):
                            ac.wait_ge(q["nodes_ready"].handle, q["nodes_ready"].at(c))
                        nc.scalar.activation(hbuf[:], bank[0][LO, :], ACT.Relu).then_inc(q["act_ready"].handle, 1)
                    chunks(ac.Fori, body)

                @block.sync
                def _(sp):
                    def body(c):
                        sp.wait_ge(q["tile_ready"].handle, q["tile_ready"].at(c + 1))
                        sp.dma_start(table_rows(node_table, c), tbuf[:]).then_inc(s_tab.handle, 16)
                    chunks(sp.Fori, body)
                    sp.wait_ge(s_tab.handle, s_tab.at(16 * NCH))
            s_tab.done(16 * NCH)
            for n in ["prod_ready", "mean_ready", "cleared", "nodes_ready", "tile_ready", "act_ready"]:
                q[n].done(NCH)

        def attend_pe(pe, k, c):
            pe.wait_ge(q["x_ready"].handle, q["x_ready"].at(c + 1))
            if due(c):
                pe.wait_ge(q["h_ready"].handle, q["h_ready"].at(c))
            pe.sem_inc(s_passed.handle, 1)
            nc.tensor.matmul(bank[4][LO, :], wm["G" + k][:], xbuf[:], start=True, stop=True
                             ).then_inc(q["hprod_ready"].handle, 1)
            pe.wait_ge(q["h_ready"].handle, q["h_ready"].at(c + 1))
            if due(c):
                pe.wait_ge(q["gtile_ready"].handle, q["gtile_ready"].at(c))
            pe.sem_inc(s_passed.handle, 1)
            nc.tensor.matmul(bank[5][0:H, :], rowsel[k][:, D:ROW], hbuf[:], start=True, stop=True)
            nc.tensor.matmul(bank[6][0:H, :], adsel[k][:], hbuf[:], start=True, stop=True)
            to_nodes(bank[7], hbuf, rowsel[k][:], ROW).then_inc(q["scored"].handle, 1)

        def attend_act(ac, c):
            ac.wait_ge(q["hprod_ready"].handle, q["hprod_ready"].at(c + 1))
            if due(c):
                ac.wait_ge(q["gtile_ready"].handle, q["gtile_ready"].at(c))
            nc.scalar.activation(hbuf[:], bank[4][LO, :], ACT.Copy).then_inc(q["h_ready"].handle, 1)

        def attend_ve(ve, c):
            ve.wait_ge(q["scored"].handle, q["scored"].at(c + 1))
            if due(16 * c):
                ve.wait_ge(s_tab.handle, s_tab.at(16 * c))
            ve.sem_inc(s_passed.handle, 1)
            nc.vector.tensor_copy(chunk(xT, slice(0, H), c), bank[5][0:H, :])
            nc.vector.tensor_copy(chunk(auxT, slice(0, H), c), bank[6][0:H, :])
            nc.vector.tensor_copy(chunk(accT, LO, c), hbuf[:])
            nc.vector.tensor_copy(chunk(accT, slice(D, ROW), c), ones[:])
            nc.vector.tensor_copy(gbuf[:], by_tile(bank[7], ROW)).then_inc(q["gtile_ready"].handle, 1)

        def attend_sp(sp):
            def body(c):
                sp.wait_ge(q["gtile_ready"].handle, q["gtile_ready"].at(c + 1))
                sp.dma_start(table_rows(gat_table, c), gbuf[:]).then_inc(s_tab.handle, 16)
            chunks(sp.Fori, body)
            sp.wait_ge(s_tab.handle, s_tab.at(16 * NCH))

        attend_sems = ["x_ready", "h_ready", "hprod_ready", "scored", "gtile_ready"]

        def gin_dense1():
            with nc.Block() as block:
                @block.vector
                def _(ve):
                    link = Chain(ve, s_ve)

                    def body(c):
                        nc.vector.tensor_copy(abuf[LO, :], chunk(accT, LO, c))
                        nc.vector.tensor_copy(abuf[D:P, :], chunk(auxT, slice(D, P), c)).then_inc(q["mean_ready"].handle, 1)
                        ve.wait_ge(q["nodes_ready"].handle, q["nodes_ready"].at(c + 1))
                        link(nc.vector.tensor_copy(ybuf[:], by_tile(bank[1])))
                        link(nc.vector.tensor_tensor(qbuf[:], ybuf[:], ybuf[:], ALU.mult))
                        nc.vector.tensor_reduce(st[:, 1, :], qbuf[:], AX, ALU.add).then_inc(q["root_asked"].handle, 1)
                        ve.wait_ge(q["root_done"].handle, q["root_done"].at(3 * c + 1))
                        link(nc.vector.tensor_scalar(st[:, 2, :], st[:, 2, :], 1e-12, None, ALU.max))
                        link(nc.vector.reciprocal(st[:, 3, :], st[:, 2, :]))
                        link(nc.vector.tensor_tensor(ybuf[:], ybuf[:], bc(st[:, 3, :], [P, TC, D], 2), ALU.mult))
                        link(nc.vector.tensor_tensor(ybuf[:], ybuf[:], tiles(c), ALU.add))
                        link(layer_norm(ve, link, ybuf, tbuf, 3 * c + 2))
                        link(nc.vector.tensor_tensor(ybuf[:], tbuf[:], by_tile(bank[2]), ALU.mult))
                        link(nc.vector.tensor_tensor(ybuf[:], ybuf[:], tbuf[:], ALU.add))
                        nxt = layer_norm(ve, link, ybuf, tbuf, 3 * c + 3)
                        nxt.then_inc(q["tile_ready"].handle, 1)
                        ve.wait_ge(q["tile_ready"].handle, q["tile_ready"].at(c + 1))
                        ve.sem_inc(s_passed.handle, 1)
                        link.mark(nc.vector.tensor_copy(tiles(c), tbuf[:]))
                        attend_ve(ve, c)
                        ve.wait_ge(q["gtile_ready"].handle, q["gtile_ready"].at(c + 1))
                    chunks(ve.Fori, body, link)

                @block.tensor
                def _(pe):
                    def body(c):
                        pe.wait_ge(q["mean_ready"].handle, q["mean_ready"].at(c + 1))
                        pe.sem_inc(s_passed.handle, 1)
                        nc.tensor.matmul(bank[0][LO, :], wm["W11"][:], abuf[LO, :], start=True, stop=True
                                         ).then_inc(q["prod_ready"].handle, 1)
                        to_nodes(bank[2], abuf[D:P, :], ident[D:P, D:P], D)
                        pe.wait_ge(q["act_ready"].handle, q["act_ready"].at(c + 1))
                        to_nodes(bank[1], hbuf, wm["W21"][:], D).then_inc(q["nodes_ready"].handle, 1)
                        pe.wait_ge(q["tile_ready"].handle, q["tile_ready"].at(c + 1))
                        for t in range(TC):
                            last = nc.tensor.matmul(bank[3][LO, t * P:(t + 1) * P], tbuf[:, t, :], ident[:],
                                                    start=True, stop=True)
                        last.then_inc(q["back_ready"].handle, 1)
                        attend_pe(pe, "1", c)
                    chunks(pe.Fori, body)

                @block.scalar
                def _(ac):
                    def body(c):
                        ac.wait_ge(q["prod_ready"].handle, q["prod_ready"].at(c + 1))
                        nc.scalar.activation(hbuf[:], bank[0][LO, :], ACT.Relu).then_inc(q["act_ready"].handle, 1)
                        root(ac, 3 * c + 1)
                        root(ac, 3 * c + 2)
                        root(ac, 3 * c + 3)
                        ac.wait_ge(q["back_ready"].handle, q["back_ready"].at(c + 1))
                        nc.scalar.activation(xbuf[:], bank[3][LO, :], ACT.Copy).then_inc(q["x_ready"].handle, 1)
                        attend_act(ac, c)
                    chunks(ac.Fori, body)

                @block.sync
                def _(sp):
                    attend_sp(sp)
            s_ve.done(s_ve.total)
            s_tab.done(16 * NCH)
            for n in attend_sems + ["prod_ready", "mean_ready", "nodes_ready", "tile_ready", "act_ready", "back_ready"]:
                q[n].done(NCH)
            for n in ["root_asked", "root_done"]:
                q[n].done(3 * NCH)

        def gat_dense(k, nxt):
            bias = col["gb" + k]
            with nc.Block() as block:
                @block.vector
                def _(ve):
                    link = Chain(ve, s_ve)

                    def body(c):
                        ve.wait_ge(q["prod_ready"].handle, q["prod_ready"].at(c + 1))
                        link(nc.vector.reciprocal(abuf[LO, :], bank[0][LO, :]))
                        nc.vector.tensor_tensor(abuf[LO, :], abuf[LO, :], chunk(accT, LO, c), ALU.mult
                                                ).then_inc(q["mean_ready"].handle, 1)
                        if nxt:
                            attend_ve(ve, c)
                            ve.wait_ge(q["gtile_ready"].handle, q["gtile_ready"].at(c + 1))
                        else:
                            ve.wait_ge(q["nodes_ready"].handle, q["nodes_ready"].at(c + 1))
                            if due(16 * c):
                                ve.wait_ge(s_tab.handle, s_tab.at(16 * c))
                            link(nc.vector.tensor_tensor(ybuf[:], by_tile(bank[1]), tiles(c), ALU.add))
                            layer_norm(ve, link, ybuf, tbuf, c + 1).then_inc(q["tile_ready"].handle, 1)
                            ve.wait_ge(q["tile_ready"].handle, q["tile_ready"].at(c + 1))
                    chunks(ve.Fori, body, link)

                @block.tensor
                def _(pe):
                    def body(c):
                        if due(c):
                            pe.wait_ge(q["gtile_ready" if nxt else "tile_ready"].handle, q["gtile_ready" if nxt else "tile_ready"].at(c))
                        nc.tensor.matmul(bank[0][LO, :], denom[:], chunk(accT, slice(0, ROW), c), start=True, stop=True
                                         ).then_inc(q["prod_ready"].handle, 1)
                        if nxt:
                            attend_pe(pe, nxt, c)
                        else:
                            pe.wait_ge(q["x_ready"].handle, q["x_ready"].at(c + 1))
                            to_nodes(bank[1], xbuf, ident[LO, LO], D).then_inc(q["nodes_ready"].handle, 1)
                    chunks(pe.Fori, body)

                @block.scalar
                def _(ac):
                    def body(c):
                        ac.wait_ge(q["mean_ready"].handle, q["mean_ready"].at(c + 1))
                        nc.scalar.activation(xbuf[:], abuf[LO, :], ACT.Relu if nxt else ACT.Identity, bias=bias
                                             ).then_inc(q["x_ready"].handle, 1)
                        if nxt:
                            attend_act(ac, c)
                        else:
                            root(ac, c + 1)
                    chunks(ac.Fori, body)

                @block.sync
                def _(sp):
                    if nxt:
                        attend_sp(sp)
                    else:
                        full = N // CH
                        with sp.Fori(0, full) as c:
                            sp.wait_ge(q["tile_ready"].handle, q["tile_ready"].at(c + 1))
                            sp.dma_start(table_rows(out, c), tbuf[:]).then_inc(s_tab.handle, 16)
                        sp.wait_ge(q["tile_ready"].handle, q["tile_ready"].at(NCH))
                        left, t, n = N - full * CH, 0, 0
                        while left > 0:
                            r = min(left, P)
                            sp.dma_start(out[full * CH + t * P:full * CH + t * P + r, :], tbuf[0:r, t, :]
                                         ).then_inc(s_tab.handle, 16)
                            left, t, n = left - r, t + 1, n + 1
                        sp.wait_ge(s_tab.handle, s_tab.at(16 * (full + n)))
            s_ve.done(s_ve.total)
            s_tab.done(16 * NCH)
            for n in ["prod_ready", "mean_ready"] + (attend_sems if nxt else ["x_ready", "nodes_ready", "tile_ready", "root_asked", "root_done"]):
                q[n].done(NCH)

        def gat_pass(name):
            s_rows = [sem(f"{name}_rows_loaded{i}") for i in range(R)]
            scoresT = [bank[0], bank[1]]
            scores = [bank[2], bank[3]]
            edge = bank[4]
            wide = bank[5]
            small = bank[6]
            HALFG = G // 2

            def is0(g):
                return isinstance(g, int) and g == 0

            with nc.Block() as block:
                @block.sync
                def _(sp):
                    def body(g, s, it):
                        if due(it * 16 * G):
                            sp.wait_ge(s_rows[s].handle, s_rows[s].at(it * 16 * G))
                        sp.dma_start(idx[s][:], A["src"][ds(g, 1), :, :].rearrange("o p j -> (o p) j")
                                     ).then_inc(s_idx[s].handle, 16)
                        if due(g - R + 1):
                            sp.wait_ge(q["edge_ready"].handle, q["edge_ready"].at(g - R + 1))
                        sp.dma_start(bufA[s][:].bitcast(I32), A["dst_rows"][ds(g, 1), :].broadcast_to([P, GE])
                                     ).then_inc(s_bA[s].handle, 16)
                    turns(body)(sp.Fori)

                @block.gpsimd
                def _(po):
                    def body(g, s, it):
                        po.wait_ge(s_idx[s].handle, s_idx[s].at(it * 16 + 16))
                        if due(g - R + 1):
                            po.wait_ge(q["msg_ready"].handle, q["msg_ready"].at(g - R + 1))
                        po.sem_inc(s_passed.handle, 1)
                        for j in range(G):
                            nc.gpsimd.indirect_dma_start(rows[s][:, j, :], None, gat_table,
                                                         bass.IndirectOffsetOnAxis(idx[s][:, j:j + 1], 0)
                                                         ).then_inc(s_rows[s].handle, 16)
                    turns(body)(po.Fori)

                @block.tensor
                def _(pe):
                    def values(g, s):
                        pe.wait_ge(q["avm_ready"].handle, q["avm_ready"].at(g + 1))
                        pe.wait_ge(q["selT_ready"].handle, q["selT_ready"].at(g + 1))
                        if due(g):
                            pe.wait_ge(q["z_done"].handle, q["z_done"].at(g))
                        for j in range(G):
                            last = nc.tensor.matmul(edge[:, j * 2 * H:(j + 1) * 2 * H], bufB[s][0:WIN, j * P:(j + 1) * P],
                                                    avm[:], start=True, stop=True)
                        last.then_inc(q["edge_ready"].handle, 1)

                    def sums(g, s):
                        pe.wait_ge(q["sel_ready"].handle, q["sel_ready"].at(g + 1))
                        pe.wait_ge(q["msg_ready"].handle, q["msg_ready"].at(g + 1))
                        for j in range(G):
                            last = nc.tensor.matmul(wide[0:ROW, 0:WIN], msg[s][:, j, :], sel[s][:, j, :],
                                                    start=j == 0, stop=j == G - 1)
                        last.then_inc(q["sum_ready"].handle, 1)

                    def body(g, s, it):
                        if not is0(g):
                            values(g - 1, (s - 1) % R)
                        pe.wait_ge(s_rows[s].handle, s_rows[s].at((it + 1) * 16 * G))
                        if due(g):
                            pe.wait_ge(q["scores8_ready"].handle, q["scores8_ready"].at(g))
                        for j in range(G):
                            last = nc.tensor.matmul(scoresT[j // HALFG][0:H, (j % HALFG) * P:(j % HALFG + 1) * P],
                                                    rows[s][:, j, D:ROW], ident[:], start=True, stop=True)
                        last.then_inc(q["scoresT_ready"].handle, 1)
                        pe.wait_ge(q["scores8_ready"].handle, q["scores8_ready"].at(g + 1))
                        if due(NSUB * 2 * g):
                            pe.wait_ge(q["max_done"].handle, q["max_done"].at(NSUB * 2 * g))
                        for h in range(2):
                            last = nc.tensor.matmul(scores[h][:], spread[:], score8[:, h * 512:(h + 1) * 512],
                                                    start=True, stop=True)
                        last.then_inc(q["scores_ready"].handle, 1)
                        if not is0(g):
                            sums(g - 1, (s - 1) % R)
                        pe.wait_ge(q["pick_ready"].handle, q["pick_ready"].at(g + 1))
                        if due(g):
                            pe.wait_ge(q["avm_ready"].handle, q["avm_ready"].at(g))
                        nc.tensor.matmul(small[0:H, 0:WIN], heads[:], subpick[:].rearrange("p a b -> p (a b)"),
                                         start=True, stop=True).then_inc(q["winmax_ready"].handle, 1)
                        pe.wait_ge(q["shift_ready"].handle, q["shift_ready"].at(g + 1))
                        nc.tensor.matmul(small[0:WIN, 64:64 + H], adw[:], ident[0:H, 0:H], start=True, stop=True)
                        nc.tensor.matmul(small[0:WIN, 64 + H:64 + 2 * H], V[:, 1, :], ident[0:H, 0:H],
                                         start=True, stop=True).then_inc(q["colsT_ready"].handle, 1)
                        pe.wait_ge(q["res_ready"].handle, q["res_ready"].at(g + 1))
                        if due(g):
                            pe.wait_ge(q["acc_done"].handle, q["acc_done"].at(g))
                        nc.tensor.matmul(wide[0:ROW, 64:64 + WIN], widen[:], res[:], start=True, stop=True
                                         ).then_inc(q["wide_ready"].handle, 1)
                    turns(body)(pe.Fori)
                    values(NG - 1, (NG - 1) % R)
                    sums(NG - 1, (NG - 1) % R)

                @block.scalar
                def _(ac):
                    def weights(g, s):
                        ac.wait_ge(q["z_done"].handle, q["z_done"].at(g + 1))
                        if due(g - R + 1):
                            ac.wait_ge(q["sum_ready"].handle, q["sum_ready"].at(g - R + 1))
                        nc.scalar.activation(msg[s][:, :, D:ROW], z[:], ACT.Exp).then_inc(q["p_ready"].handle, 1)

                    def body(g, s, it):
                        ac.wait_ge(s_bA[s].handle, s_bA[s].at(it * 16 + 16))
                        ac.wait_ge(q["cols_ready"].handle, q["cols_ready"].at(g + 1))
                        for k in range(NSUB):
                            if not is0(g):
                                ac.wait_ge(q["max_done"].handle, q["max_done"].at(2 * (NSUB * (g - 1) + k + 1)))
                            nc.scalar.activation(far[k][:], bufA[s][:].bitcast(I32), ACT.Square, bias=subcol[:, k:k + 1],
                                                 scale=BIG).then_inc(q["far_ready"].handle, 1)
                        if not is0(g):
                            weights(g - 1, (s - 1) % R)
                        ac.wait_ge(q["scoresT_ready"].handle, q["scoresT_ready"].at(g + 1))
                        if due(g):
                            ac.wait_ge(q["scores_ready"].handle, q["scores_ready"].at(g))
                        for h in range(2):
                            last = nc.scalar.activation(score8[:, h * 512:(h + 1) * 512], scoresT[h][0:H, :], ACT.Copy)
                        last.then_inc(q["scores8_ready"].handle, 1)
                        ac.wait_ge(q["shift_ready"].handle, q["shift_ready"].at(g + 1))
                        if due(g):
                            ac.wait_ge(q["wide_ready"].handle, q["wide_ready"].at(g))
                        nc.scalar.activation(res[:], dif[:], ACT.Exp).then_inc(q["res_ready"].handle, 1)
                        ac.wait_ge(q["colsT_ready"].handle, q["colsT_ready"].at(g + 1))
                        if due(g):
                            ac.wait_ge(q["edge_ready"].handle, q["edge_ready"].at(g))
                        nc.scalar.activation(avm[:], small[0:WIN, 64:64 + 2 * H], ACT.Copy).then_inc(q["avm_ready"].handle, 1)
                    turns(body)(ac.Fori)
                    weights(NG - 1, (NG - 1) % R)

                @block.vector
                def _(ve):
                    link = Chain(ve, s_ve)

                    def messages(g, s):
                        ve.wait_ge(q["edge_ready"].handle, q["edge_ready"].at(g + 1))
                        if due(g):
                            ve.wait_ge(q["p_ready"].handle, q["p_ready"].at(g))
                        ed = edge[:, 0:G * 2 * H].rearrange("p (j v) -> p j v", v=2 * H)
                        link(nc.vector.tensor_tensor(z[:], rows[s][:, :, D:ROW], ed[:, :, 0:H], ALU.add))
                        link(nc.vector.scalar_tensor_tensor(z[:], z[:], SLOPE, z[:], ALU.mult, ALU.max))
                        link(nc.vector.tensor_tensor(z[:], z[:], ed[:, :, H:2 * H], ALU.subtract))
                        nc.vector.tensor_scalar(z[:], z[:], 0.0, None, ALU.min).then_inc(q["z_done"].handle, 1)
                        ve.wait_ge(q["p_ready"].handle, q["p_ready"].at(g + 1))
                        nc.vector.tensor_tensor(msg[s][:, :, 0:D].rearrange("p j (h c) -> p j h c", c=C),
                                                rows[s][:, :, 0:D].rearrange("p j (h c) -> p j h c", c=C),
                                                bc(msg[s][:, :, D:ROW], [P, G, H, C], 3), ALU.mult
                                                ).then_inc(q["msg_ready"].handle, 1)

                    def add_sums(g, s):
                        base = ve.value_load(first_i[0:1, ds(g, 1)], min_val=0, max_val=N)
                        w = accT[0:ROW, ds(base, WIN)]
                        ve.wait_ge(q["wide_ready"].handle, q["wide_ready"].at(g + 1))
                        ve.wait_ge(q["sum_ready"].handle, q["sum_ready"].at(g + 1))
                        if due(g):
                            ve.wait_ge(q["acc_done"].handle, q["acc_done"].at(g))
                        link(nc.vector.tensor_tensor(w, w, wide[0:ROW, 64:64 + WIN], ALU.mult))
                        nc.vector.tensor_tensor(w, w, wide[0:ROW, 0:WIN], ALU.add).then_inc(q["acc_done"].handle, 1)

                    def body(g, s, it):
                        if due(NSUB * g):
                            ve.wait_ge(q["far_ready"].handle, q["far_ready"].at(NSUB * g))
                        base_col = first[:, ds(g, 1)]
                        link.mark(nc.vector.tensor_scalar(stcol[:], part[:], base_col, None, ALU.add))
                        nc.vector.tensor_scalar(subcol[:], subnode[:], base_col, -BIG, ALU.add, ALU.mult
                                                ).then_inc(q["cols_ready"].handle, 1)
                        ve.wait_ge(s_bA[s].handle, s_bA[s].at(it * 16 + 16))
                        if due(g - R + 1):
                            ve.wait_ge(q["edge_ready"].handle, q["edge_ready"].at(g - R + 1))
                        link.join()
                        nc.vector.tensor_scalar(bufB[s][0:WIN, :], bufA[s][0:WIN, :].bitcast(I32), stcol[0:WIN, :], None,
                                                ALU.is_equal).then_inc(q["selT_ready"].handle, 1)
                        if due(g - R + 1):
                            ve.wait_ge(q["sum_ready"].handle, q["sum_ready"].at(g - R + 1))
                        nc.vector.tensor_tensor(sel[s][:], bc(iota[:], [P, G, WIN], 1),
                                                bc(drel[:, ds(g, 1), :].rearrange("p o j -> p (o j)"), [P, G, WIN], 2),
                                                ALU.is_equal).then_inc(q["sel_ready"].handle, 1)
                        if not is0(g):
                            messages(g - 1, (s - 1) % R)
                        ve.wait_ge(q["scores_ready"].handle, q["scores_ready"].at(g + 1))
                        for k in range(NSUB):
                            ve.wait_ge(q["far_ready"].handle, q["far_ready"].at(NSUB * g + k + 1))
                            ve.sem_inc(s_passed.handle, 1)
                            for h in range(2):
                                nc.vector.tensor_tensor_reduce(
                                    out=far[k][:, h * 512:(h + 1) * 512], in0=scores[h][:], in1=far[k][:, h * 512:(h + 1) * 512],
                                    scale=1.0, scalar=-3.0e38, op0=ALU.subtract, op1=ALU.max,
                                    accum_out=submax2[:, k, h:h + 1]).then_inc(q["max_done"].handle, 1)
                        ve.wait_ge(q["max_done"].handle, q["max_done"].at(NSUB * 2 * (g + 1)))
                        link(nc.vector.tensor_reduce(submax[:], submax2[:], AX, ALU.max))
                        nc.vector.tensor_tensor(subpick[:], bc(submax[:], [P, NSUB, SUB], 2), bc(pick[:], [P, NSUB, SUB], 1),
                                                ALU.mult).then_inc(q["pick_ready"].handle, 1)
                        if not is0(g):
                            add_sums(g - 1, (s - 1) % R)
                        base = ve.value_load(first_i[0:1, ds(g, 1)], min_val=0, max_val=N)
                        m = xT[0:H, ds(base, WIN)]
                        a = auxT[0:H, ds(base, WIN)]
                        if due(g):
                            ve.wait_ge(q["colsT_ready"].handle, q["colsT_ready"].at(g))
                        if due(g):
                            ve.wait_ge(q["res_ready"].handle, q["res_ready"].at(g))
                        link.mark(nc.vector.tensor_copy(adw[:], a))
                        link(nc.vector.tensor_tensor(U[:, 0, :], m, a, ALU.add))
                        ve.wait_ge(q["winmax_ready"].handle, q["winmax_ready"].at(g + 1))
                        link(nc.vector.tensor_tensor(m, m, small[0:H, 0:WIN], ALU.max))
                        link(nc.vector.tensor_tensor(U[:, 1, :], m, a, ALU.add))
                        link(nc.vector.scalar_tensor_tensor(V[:], U[:], SLOPE, U[:], ALU.mult, ALU.max))
                        nc.vector.tensor_tensor(dif[:], V[:, 0, :], V[:, 1, :], ALU.subtract).then_inc(q["shift_ready"].handle, 1)

                    body(0, 0, 0)
                    n0 = link.close()
                    link.offset = n0
                    body(1, 1, 0)
                    n1 = link.close()
                    link.offset = n0 + n1
                    body(2, 2, 0)
                    link.close()
                    with ve.Fori(1, NG // R) as it:
                        for s in range(R):
                            link.offset = n0 + n1 * (it * R + s - 1)
                            body(it * R + s, s, it)
                            assert link.close() == n1
                    for g in range(R * (NG // R), NG):
                        link.offset = n0 + n1 * (g - 1)
                        body(g, g % R, g // R)
                        link.close()
                    link.offset = n0 + n1 * (NG - 1)
                    messages(NG - 1, (NG - 1) % R)
                    add_sums(NG - 1, (NG - 1) % R)
                    s_ve.total = link.offset + link.close()
            s_ve.done(s_ve.total)
            for s in range(R):
                s_idx[s].done(16 * slot_total(s))
                s_bA[s].done(16 * slot_total(s))
            for n in ["avm_ready", "selT_ready", "z_done", "edge_ready", "sel_ready", "msg_ready", "sum_ready", "scoresT_ready",
                      "scores8_ready", "scores_ready", "pick_ready", "winmax_ready", "shift_ready", "colsT_ready", "res_ready",
                      "acc_done", "wide_ready", "p_ready", "cols_ready"]:
                q[n].done(NG)
            q["max_done"].done(2 * NSUB * NG)
            q["far_ready"].done(NSUB * NG)
            gat_further(name)

        sum_pass("sage0", A["x"], attr=True, aux=True)
        sage_dense(0)
        sum_pass("sage1", node_table, attr=True)
        sage_dense(1)
        sum_pass("sage2", node_table, attr=True)
        sage_dense(2)
        sum_pass("gin0", node_table)
        gin_dense0()
        sum_pass("gin1", node_table)
        gin_dense1()
        gat_pass("gat0")
        gat_dense("1", "3")
        gat_pass("gat1")
        gat_dense("3", "2")
        gat_pass("gat2")
        gat_dense("2", None)


def constants():
    p = np.arange(P)
    f = np.float32
    c = {"c_ident": np.eye(P, dtype=f), "c_iota": np.tile(np.arange(WIN, dtype=f), (P, 1)), "c_part": p[:, None].astype(f)}
    c["c_subnode"] = (p[:, None] // H + SUB * np.arange(NSUB)[None]).astype(f)
    c["c_pick"] = (p[:, None] // H == np.arange(SUB)[None]).astype(f)
    c["c_heads"] = (p[:, None] % H == np.arange(H)[None]).astype(f)
    c["c_spread"] = np.ascontiguousarray(c["c_heads"].T)
    w = np.zeros((H, ROW), f)
    for h in range(H):
        w[h, h * C:(h + 1) * C] = 1
        w[h, D + h] = 1
    c["c_widen"] = w
    d = np.zeros((ROW, D), f)
    for h in range(H):
        d[D + h, h * C:(h + 1) * C] = 1
    c["c_denom"] = d
    c["c_blk"] = (np.arange(D)[:, None] // C == np.arange(H)[None]).astype(f)
    return c


def lay_out(inputs):
    a = {k: np.asarray(v) for k, v in inputs.items()}
    pad = lambda v, fill: np.concatenate([v, np.full((EP - E,) + v.shape[1:], fill, v.dtype)])
    o = constants()
    o["src"] = pad(a["src"], 0).reshape(NG, P, G)
    dst = pad(a["dst"], N).reshape(NG, P, G)
    o["dst"] = np.ascontiguousarray(dst.transpose(1, 0, 2)).reshape(P, NG * G)
    o["dst_rows"] = np.ascontiguousarray(dst.transpose(0, 2, 1)).reshape(NG, GE)
    o["wgt"] = np.ascontiguousarray(pad(a["edge_weight"], 0).reshape(NG, P, G).transpose(1, 0, 2))
    o["attr16"] = np.ascontiguousarray(pad(a["edge_attr_16"], 0).reshape(NG, P, G, EA).transpose(0, 3, 2, 1)).reshape(NG, EA, GE)
    o["attr64"] = pad(a["edge_attr_64"], 0).reshape(NG, P, G * D)
    o["x"] = np.concatenate([a["x"], np.zeros((NP - N, D), a["x"].dtype)])
    o["emb"] = a["L0_gnn_emb_ea"]
    for i in range(3):
        o[f"Wl{i}"], o[f"Wr{i}"] = a[f"L0_gnn_Wl{i}"], a[f"L0_gnn_Wr{i}"]
    for i in range(2):
        o[f"W1{i}"], o[f"W2{i}"] = a[f"L1_gnn_W1_{i}"].T, a[f"L1_gnn_W2_{i}"].T
    for k in "132":
        o["G" + k] = a["L3_gnn_W" + k].T
    c = [a["L0_gnn_bl0"], a["L0_gnn_bl1"], a["L0_gnn_bl2"], a["L3_gnn_b1"], a["L3_gnn_b3"], a["L3_gnn_b2"]]
    for k in "132":
        c += [a["L3_gnn_as" + k].reshape(D), a["L3_gnn_ad" + k].reshape(D)]
    o["cols"] = np.stack(c, 1)
    return {k: np.ascontiguousarray(v) for k, v in o.items()}


def kernel(**inputs):
    import concourse.bacc as bacc
    from concourse.bass_utils import run_bass_kernel_spmd

    nc = bacc.Bacc("TRN2", target_bir_lowering=False, num_devices=1)
    arrays = lay_out(inputs)
    aps = {k: nc.dram_tensor("in_" + k, v.shape, mybir.dt.from_np(v.dtype), kind="ExternalInput").ap()
           for k, v in arrays.items()}
    out = nc.dram_tensor("out", (N, D), F32, kind="ExternalOutput").ap()
    build(nc, aps, out)
    r = run_bass_kernel_spmd(nc, [{"in_" + k: v for k, v in arrays.items()}], core_ids=[0])
    return r.results[0]["out"]
```

```python
import numpy as np
import concourse.bass as bass
from concourse import mybir
from concourse.alu_op_type import AluOpType as ALU
from contextlib import ExitStack

F32 = mybir.dt.float32
I32 = mybir.dt.int32
ACT = mybir.ActivationFunctionType
AX = mybir.AxisListType.X

N, E, D, EA, H, C = 6250, 206250, 64, 16, 8, 8
P = 128
G = 8
GE = G * P
NG = -(-E // GE)
EP = NG * GE
CH = 512
NCH = -(-(N + 64) // CH)
NP = NCH * CH
TC = CH // P
WIN = 48
SUB = P // H
NSUB = WIN // SUB
R = 3
RG = 4
ROW = D + H
BIG = float(2 ** 50)
EPS = 1e-5
SLOPE = 0.2
HALF = 101
assert NG == 2 * HALF and R * (NG // R) < NG and RG * (NG // RG) < NG and N % 2 == 0


def ds(start, size):
    return bass.ds(start, size)


def bc(ap, shape, axis):
    return ap.unsqueeze(axis).broadcast_to(shape)


class Sem:

    def __init__(self, handle):
        self.handle, self.base = handle, 0

    def at(self, count):
        return self.base + count

    def done(self, total):
        self.base += total


def due(count):
    return not isinstance(count, int) or count > 0


class Chain:

    def __init__(self, engine, sem):
        self.engine, self.sem, self.n, self.offset, self.per = engine, sem, 0, 0, 0

    def __call__(self, ins):
        self.n += 1
        ins.then_inc(self.sem.handle, 1)
        self.engine.wait_ge(self.sem.handle, self.sem.at(self.offset + self.n))

    def mark(self, ins):
        self.n += 1
        ins.then_inc(self.sem.handle, 1)

    def join(self):
        self.engine.wait_ge(self.sem.handle, self.sem.at(self.offset + self.n))

    def close(self):
        n, self.n = self.n, 0
        return n


def build(nc, A, out):
    ctx = ExitStack()
    with ctx:
        def sb(name, shape, dt=F32):
            return ctx.enter_context(nc.sbuf_tensor(name, shape, dt))

        def sem(name):
            return Sem(ctx.enter_context(nc.semaphore(name)))

        def dram(name, shape):
            return nc.dram_tensor(name, shape, F32, kind="Internal").ap()

        node_table = dram("node_table", (NP, D))
        gat_table = dram("gat_table", (NP, ROW))

        accT = sb("accT", [P, NP])
        auxT = sb("auxT", [P, NP])
        xT = sb("xT", [P, NP])
        X = sb("X", [P, NP // P, D])
        drel = sb("drel", [P, NG, G])
        wgt = sb("wgt", [P, NG, G])
        first = sb("first", [P, NG])
        first_i = sb("first_i", [1, NG], I32)
        span_i = sb("span_i", [1, NG], I32)
        widest = sb("widest", [1, 1])
        widest_i = sb("widest_i", [1, 1], I32)
        shift = sb("shift", [P, 1])
        base_col = sb("base_col", [P, 1])
        far_rel = sb("far_rel", [P, G])
        ident = sb("ident", [P, P])
        iota = sb("iota", [P, WIN])
        part = sb("part", [P, 1])
        subnode = sb("subnode", [P, NSUB])
        pick = sb("pick", [P, SUB])
        heads = sb("heads", [P, H])
        widen = sb("widen", [H, ROW])
        denom = sb("denom", [ROW, D])
        blk = sb("blk", [D, H])
        emb = sb("emb", [EA, D])
        names64 = ["Wl0", "Wr0", "Wl1", "Wr1", "Wl2", "Wr2", "W10", "W20", "W11", "W21", "G1", "G3", "G2"]
        wm = {n: sb(f"w_{n}", [D, D]) for n in names64}
        colnames = ["bl0", "bl1", "bl2", "gb1", "gb3", "gb2", "as1", "ad1", "as3", "ad3", "as2", "ad2"]
        cols = sb("cols", [D, len(colnames)])
        col = {n: cols[:, i:i + 1] for i, n in enumerate(colnames)}
        rowsel = {k: sb(f"rowsel{k}", [D, ROW]) for k in "132"}
        adsel = {k: sb(f"adsel{k}", [D, H]) for k in "132"}
        zeros = sb("zeros", [P, CH])
        ones = sb("ones", [H, CH])
        idx = [sb(f"idx{i}", [P, G], I32) for i in range(RG)]
        rows = [sb(f"rows{i}", [P, G, ROW]) for i in range(RG)]
        bufA = [sb(f"bufA{i}", [P, GE]) for i in range(RG)]
        bufB = [sb(f"bufB{i}", [P, GE]) for i in range(RG)]
        sel = [sb(f"sel{i}", [P, G, WIN]) for i in range(RG)]
        msg = [sb(f"msg{i}", [P, G, ROW]) for i in range(RG)]
        far = [sb(f"far{i}", [P, GE]) for i in range(NSUB)]
        rep = sb("rep", [P, G, P])
        subcol = sb("subcol", [P, NSUB])
        stcol = sb("stcol", [P, 1])
        submax2 = sb("submax2", [P, NSUB, 2])
        submax = sb("submax", [P, NSUB])
        subpick = sb("subpick", [P, NSUB, SUB])
        U = sb("U", [H, 2, WIN])
        V = sb("V", [H, 2, WIN])
        dif = sb("dif", [H, WIN])
        adw = sb("adw", [H, WIN])
        res = sb("res", [H, WIN])
        avm = sb("avm", [WIN, 2 * H])
        z = sb("z", [P, G, H])
        zpos = sb("zpos", [P, G, H])
        abuf = sb("abuf", [P, CH])
        hbuf = sb("hbuf", [D, CH])
        xbuf = sb("xbuf", [D, CH])
        tbuf = sb("tbuf", [P, TC, D])
        gbuf = sb("gbuf", [P, TC, ROW])
        ybuf = sb("ybuf", [P, TC, D])
        qbuf = sb("qbuf", [P, TC, D])
        st = sb("st", [P, 4, TC])

        scores = ctx.enter_context(nc.psum_tensor("scores", [P, GE], F32))
        bank = {i: ctx.enter_context(nc.psum_tensor(f"bank{i}", [P, 512], F32)) for i in [0, 1, 4, 5, 6, 7]}
        bank[2], bank[3] = scores[:, 0:512], scores[:, 512:1024]

        s_load = sem("inputs_loaded")
        s_ve = sem("vector_chain")
        s_ac = sem("scalar_done")
        s_pe = sem("tensor_done")
        s_po = sem("pool_done")
        s_tab = sem("table_written")
        s_out = sem("output_written")
        s_passed = sem("waits_passed")
        s_idx = [sem(f"idx_loaded{i}") for i in range(RG)]
        s_bA = [sem(f"bufA_loaded{i}") for i in range(RG)]
        s_bB = [sem(f"bufB_loaded{i}") for i in range(R)]
        names = ["rows_free", "ea_ready", "sum_ready", "aux_ready", "sel_ready", "pre_ready", "msg_ready", "acc_done",
                 "auxacc_done", "rep_ready", "scores_ready", "cols_ready", "far_ready", "max_done",
                 "pick_ready", "winmax_ready", "shift_ready", "colsT_ready", "avm_ready", "res_ready", "wide_ready",
                 "edge_ready", "z_done", "zpos_ready", "p_ready", "selT_ready",
                 "once", "prod_ready", "mean_ready", "cleared", "nodes_ready", "tile_ready", "x_ready", "act_ready", "kept",
                 "root_asked", "root_done", "h_ready", "hprod_ready", "scored", "gtile_ready", "back_ready"]
        q = {n: sem(n) for n in names}

        loads = [(ident[:], A["c_ident"]), (iota[:], A["c_iota"]), (part[:], A["c_part"]), (subnode[:], A["c_subnode"]),
                 (pick[:], A["c_pick"]), (heads[:], A["c_heads"]), (widen[:], A["c_widen"]),
                 (denom[:], A["c_denom"]), (blk[:], A["c_blk"]), (emb[:], A["emb"]), (wgt[:], A["wgt"]),
                 (X[:], A["x"].rearrange("(t p) d -> p t d", p=P)),
                 (cols[:], A["cols"])]
        loads += [(wm[n][:], A[n]) for n in names64]
        group_dst = accT[0:HALF, 0:2 * GE].bitcast(I32)
        dst_i = auxT[:, 0:NG * G].bitcast(I32)
        with nc.Block() as block:
            @block.sync
            def _(sp):
                sp.dma_start(group_dst.rearrange("p (h e) -> p h e", h=2),
                             A["dst_rows"].rearrange("(h p) e -> p h e", p=HALF)).then_inc(s_load.handle, 16)
                sp.dma_start(dst_i, A["dst"]).then_inc(s_load.handle, 16)
                for o, i in loads:
                    sp.dma_start(o, i).then_inc(s_load.handle, 16)

            @block.vector
            def _(ve):
                link = Chain(ve, s_ve)
                ve.wait_ge(s_load.handle, s_load.at(16 * (len(loads) + 2)))
                ends = st[0:HALF, 0:2, 0:2]
                for h in range(2):
                    src = group_dst[:, h * GE:(h + 1) * GE]
                    link.mark(nc.vector.tensor_reduce(ends[:, 0, h:h + 1], src, AX, ALU.min))
                    link.mark(nc.vector.tensor_reduce(ends[:, 1, h:h + 1], src, AX, ALU.max))
                link.join()
                for e in range(2):
                    for h in range(2):
                        link.mark(nc.vector.tensor_scalar(abuf[0:HALF, (2 * e + h) * HALF:(2 * e + h + 1) * HALF],
                                                          ident[0:HALF, 0:HALF], ends[:, e, h:h + 1], None, ALU.mult))
                link.mark(nc.vector.memset(ybuf[:], 1.0))
                link.mark(nc.vector.memset(zeros[:], 0.0))
                link.mark(nc.vector.memset(ones[:], 1.0))
                for i in range(R):
                    link.mark(nc.vector.memset(bufA[i][:], 1.0))
                for k in "132":
                    link.mark(nc.vector.tensor_copy(rowsel[k][:, 0:D], ident[0:D, 0:D]))
                    link.mark(nc.vector.tensor_scalar(rowsel[k][:, D:ROW], blk[:], col["as" + k], None, ALU.mult))
                    link.mark(nc.vector.tensor_scalar(adsel[k][:], blk[:], col["ad" + k], None, ALU.mult))
                link.join()
                ve.wait_ge(s_pe.handle, s_pe.at(1))
                link(nc.vector.tensor_copy(first[:], bank[0][:, 0:NG]))
                link(nc.vector.tensor_copy(first_i[:], bank[0][0:1, 0:NG]))
                link(nc.vector.tensor_copy(span_i[:], bank[0][0:1, NG:2 * NG]))
                link(nc.vector.tensor_tensor(span_i[:], span_i[:], first_i[:], ALU.subtract))
                link(nc.vector.tensor_reduce(widest[:], span_i[:], AX, ALU.max))
                link(nc.vector.tensor_copy(widest_i[:], widest[:]))
                link(nc.vector.tensor_copy(drel[:].rearrange("p g j -> p (g j)"), dst_i))
                link(nc.vector.tensor_tensor(drel[:], drel[:], bc(first[:], [P, NG, G], 2), ALU.subtract))
                link(nc.vector.memset(accT[:], 0.0))
                link(nc.vector.memset(auxT[:], 0.0))
                if due(1 + NP // P):
                    ve.wait_ge(s_pe.handle, s_pe.at(1 + NP // P))
                s_ve.total = link.close()

            @block.tensor
            def _(pe):
                pe.wait_ge(s_ve.handle, s_ve.at(4 + 4 + 3 + R + 9))
                all_ones = ybuf[0:HALF, 0:2, :].rearrange("p a b -> p (a b)")
                nc.tensor.matmul(bank[0][:, 0:4 * HALF], all_ones, abuf[0:HALF, 0:4 * HALF],
                                 start=True, stop=True).then_inc(s_pe.handle, 1)
                for t in range(NP // P):
                    b = 1 + t % 2
                    if due(t - 1):
                        pe.wait_ge(s_ac.handle, s_ac.at(t - 1))
                    nc.tensor.matmul(bank[b][0:D, 0:P], X[:, t, :], ident[:], start=True, stop=True).then_inc(s_pe.handle, 1)

            @block.scalar
            def _(ac):
                for t in range(NP // P):
                    ac.wait_ge(s_pe.handle, s_pe.at(t + 2))
                    nc.scalar.activation(xT[0:D, t * P:(t + 1) * P], bank[1 + t % 2][0:D, 0:P],
                                         ACT.Copy).then_inc(s_ac.handle, 1)
        s_ve.done(s_ve.total)
        s_pe.done(1 + NP // P)
        s_ac.done(NP // P)

        def turns(body, R=R):
            for g in range(R):
                body(g, g, 0)

            def rest(fori):
                with fori(1, NG // R) as it:
                    for s in range(R):
                        body(it * R + s, s, it)
                for g in range(R * (NG // R), NG):
                    body(g, g % R, g // R)
            return rest

        def slot_total(s, R=R):
            return NG // R + (s < NG % R)

        token_vector_vector = sem("token_vector_to_vector")
        token_vector_scalar = sem("token_vector_to_scalar")
        token_scalar_vector = sem("token_scalar_to_vector")
        token_vector_tensor = sem("token_vector_to_tensor")
        token_tensor_vector = sem("token_tensor_to_vector")
        token_tensor_scalar = sem("token_tensor_to_scalar")
        token_scalar_tensor = sem("token_scalar_to_tensor")

        def settle(ve, ins):
            ins.then_inc(token_vector_vector.handle, 1)
            ve.wait_ge(token_vector_vector.handle, 1)
            ve.sem_clear(token_vector_vector.handle)

        def further(engine, group, window=None, closing=None):
            widest_reg = engine.value_load(widest_i[0:1, 0:1], min_val=0, max_val=N)
            with engine.If(widest_reg >= WIN):
                with engine.Fori(0, NG) as g:
                    group(g)
                    if window is not None:
                        span = engine.value_load(span_i[0:1, ds(g, 1)], min_val=0, max_val=N)
                        start = engine.value_load(first_i[0:1, ds(g, 1)], min_val=0, max_val=N)
                        with engine.If(span >= WIN):
                            with engine.Fori(1, span // WIN + 1) as k:
                                window(g, k, start + k * WIN)
                    if closing is not None:
                        closing(g)
                engine.nop()

        def next_window(ve, g):
            settle(ve, nc.vector.tensor_scalar(shift[:], shift[:], float(WIN), None, ALU.add))
            settle(ve, nc.vector.tensor_scalar(far_rel[:], drel[:, ds(g, 1), :].rearrange("p o j -> p (o j)"), shift[:],
                                               None, ALU.subtract))
            return nc.vector.tensor_tensor(sel[0][:], bc(iota[:], [P, G, WIN], 1), bc(far_rel[:], [P, G, WIN], 2),
                                           ALU.is_equal)

        def sum_further(name, table, attr, aux):
            f_load, f_rows, f_ea, f_done = (sem(f"{name}_further_{n}") for n in ["loaded", "rows_loaded", "ea_ready", "group_done"])
            n_load = 1 + attr + aux
            with nc.Block() as block:
                @block.sync
                def _(sp):
                    def group(g):
                        sp.wait_ge(f_done.handle, g + 1)
                        sp.dma_start(idx[0][:], A["src"][ds(g, 1), :, :].rearrange("o p j -> (o p) j")
                                     ).then_inc(f_load.handle, 16)
                        if attr:
                            sp.dma_start(bufB[0][0:EA, :], A["attr16"][ds(g, 1), :, :].rearrange("o k e -> (o k) e")
                                         ).then_inc(f_load.handle, 16)
                        if aux:
                            sp.dma_start(bufA[0][:].rearrange("p (j d) -> p j d", d=P)[:, :, D:P],
                                         A["attr64"][ds(g, 1), :, :].rearrange("o p (j d) -> (o p) j d", d=D)
                                         ).then_inc(f_load.handle, 16)
                    further(sp, group)

                @block.gpsimd
                def _(po):
                    def group(g):
                        po.wait_ge(f_load.handle, f_load.at((g + 1) * 16 * n_load))
                        po.sem_inc(s_passed.handle, 1)
                        for j in range(G):
                            nc.gpsimd.indirect_dma_start(rows[0][:, j, 0:D], None, table,
                                                         bass.IndirectOffsetOnAxis(idx[0][:, j:j + 1], 0)
                                                         ).then_inc(f_rows.handle, 16)
                    further(po, group)

                @block.tensor
                def _(pe):
                    def group(g):
                        pe.wait_ge(f_load.handle, (g + 1) * 16 * n_load)
                        if attr:
                            for j in range(G):
                                last = nc.tensor.matmul(bank[0][:, j * D:(j + 1) * D], bufB[0][0:EA, j * P:(j + 1) * P],
                                                        emb[:], start=True, stop=True)
                            last.then_inc(f_ea.handle, 1)

                    def window(g, k, start):
                        pe.wait_ge(token_vector_tensor.handle, 1)
                        pe.sem_clear(token_vector_tensor.handle)
                        if aux:
                            for j in range(G):
                                nc.tensor.matmul(bank[6][:, 0:WIN], bufA[0][:, j * P:(j + 1) * P], sel[0][:, j, :],
                                                 start=j == 0, stop=j == G - 1)
                        for j in range(G):
                            last = nc.tensor.matmul(bank[3][0:D, 0:WIN], msg[0][:, j, 0:D], sel[0][:, j, :],
                                                    start=j == 0, stop=j == G - 1)
                        last.then_inc(token_tensor_vector.handle, 1)
                    further(pe, group, window)

                @block.vector
                def _(ve):
                    nc.vector.memset(shift[:], 0.0).then_inc(f_done.handle, 1)

                    def group(g):
                        ve.wait_ge(f_rows.handle, (g + 1) * 16 * G)
                        if attr:
                            ve.wait_ge(f_ea.handle, g + 1)
                            summed = far[0][:, 0:G * D].rearrange("p (j d) -> p j d", d=D)
                            settle(ve, nc.vector.tensor_tensor(summed, rows[0][:, :, 0:D],
                                                               bank[0][:].rearrange("p (j d) -> p j d", d=D), ALU.add))
                            settle(ve, nc.vector.tensor_scalar(msg[0][:, :, 0:D], summed, 0.0, None, ALU.max))
                        else:
                            settle(ve, nc.vector.tensor_tensor(msg[0][:, :, 0:D], rows[0][:, :, 0:D],
                                                               bc(wgt[:, ds(g, 1), :].rearrange("p o j -> p (o j)"), [P, G, D], 2),
                                                               ALU.mult))
                        settle(ve, nc.vector.memset(shift[:], 0.0))

                    def window(g, k, start):
                        next_window(ve, g).then_inc(token_vector_tensor.handle, 1)
                        ve.wait_ge(token_tensor_vector.handle, 1)
                        ve.sem_clear(token_tensor_vector.handle)
                        start = nc.s_assert_within(start, 0, N, skip_runtime_bounds_check_because="a window starts at or below the last destination")
                        w = accT[0:D, ds(start, WIN)]
                        settle(ve, nc.vector.tensor_tensor(w, w, bank[3][0:D, 0:WIN], ALU.add))
                        if aux:
                            w = auxT[:, ds(start, WIN)]
                            settle(ve, nc.vector.tensor_tensor(w, w, bank[6][:, 0:WIN], ALU.add))

                    def closing(g):
                        nc.vector.memset(base_col[:], 0.0).then_inc(f_done.handle, 1)
                    further(ve, group, window, closing)

        def gat_further(name):
            f_load, f_rows, f_scores, f_done, f_rep = (sem(f"{name}_further_{n}") for n in
                                                     ["loaded", "rows_loaded", "scores_ready", "group_done", "scores_repeated"])
            with nc.Block() as block:
                @block.sync
                def _(sp):
                    def group(g):
                        sp.wait_ge(f_done.handle, g + 1)
                        sp.dma_start(idx[0][:], A["src"][ds(g, 1), :, :].rearrange("o p j -> (o p) j")
                                     ).then_inc(f_load.handle, 16)
                        sp.dma_start(bufA[0][:].bitcast(I32), A["dst_rows"][ds(g, 1), :].broadcast_to([P, GE])
                                     ).then_inc(f_load.handle, 16)
                    further(sp, group)

                @block.gpsimd
                def _(po):
                    def group(g):
                        po.wait_ge(f_load.handle, f_load.at((g + 1) * 32))
                        po.sem_inc(s_passed.handle, 1)
                        for j in range(G):
                            nc.gpsimd.indirect_dma_start(rows[0][:, j, :], None, gat_table,
                                                         bass.IndirectOffsetOnAxis(idx[0][:, j:j + 1], 0)
                                                         ).then_inc(f_rows.handle, 16)
                    further(po, group)

                @block.tensor
                def _(pe):
                    def group(g):
                        pe.wait_ge(f_rep.handle, g + 1)
                        for j in range(G):
                            last = nc.tensor.transpose(scores[:, j * P:(j + 1) * P], rep[:, j, :], ident[:])
                        last.then_inc(f_scores.handle, 1)

                    def window(g, k, start):
                        pe.wait_ge(token_vector_tensor.handle, 1)
                        pe.sem_clear(token_vector_tensor.handle)
                        nc.tensor.matmul(bank[6][0:H, 0:WIN], heads[:], subpick[:].rearrange("p a b -> p (a b)"),
                                              start=True, stop=True).then_inc(token_tensor_vector.handle, 1)
                        pe.wait_ge(token_vector_tensor.handle, 1)
                        pe.sem_clear(token_vector_tensor.handle)
                        nc.tensor.matmul(bank[6][0:WIN, 64:64 + H], adw[:], ident[0:H, 0:H], start=True, stop=True)
                        nc.tensor.matmul(bank[6][0:WIN, 64 + H:64 + 2 * H], V[:, 1, :], ident[0:H, 0:H],
                                              start=True, stop=True).then_inc(token_tensor_scalar.handle, 1)
                        pe.wait_ge(token_scalar_tensor.handle, 1)
                        pe.sem_clear(token_scalar_tensor.handle)
                        nc.tensor.matmul(bank[5][0:ROW, 64:64 + WIN], widen[:], res[:], start=True, stop=True)
                        for j in range(G):
                            last = nc.tensor.matmul(bank[4][:, j * 2 * H:(j + 1) * 2 * H], bufB[0][0:WIN, j * P:(j + 1) * P],
                                                    avm[:], start=True, stop=True)
                        last.then_inc(token_tensor_vector.handle, 1)
                        pe.wait_ge(token_vector_tensor.handle, 1)
                        pe.sem_clear(token_vector_tensor.handle)
                        for j in range(G):
                            last = nc.tensor.matmul(bank[5][0:ROW, 0:WIN], msg[0][:, j, :], sel[0][:, j, :],
                                                    start=j == 0, stop=j == G - 1)
                        last.then_inc(token_tensor_vector.handle, 1)
                    further(pe, group, window)

                @block.scalar
                def _(ac):
                    def group(g):
                        ac.wait_ge(f_rows.handle, (g + 1) * 16 * G)
                        ac.sem_inc(s_passed.handle, 1)
                        nc.scalar.activation(rep[:].rearrange("p j (a h) -> p j a h", h=H),
                                             bc(rows[0][:, :, D:ROW], [P, G, SUB, H], 2), ACT.Copy
                                             ).then_inc(f_rep.handle, 1)

                    def window(g, k, start):
                        ac.wait_ge(token_vector_scalar.handle, 1)
                        ac.sem_clear(token_vector_scalar.handle)
                        for n in range(NSUB):
                            last = nc.scalar.activation(far[n][:], bufA[0][:].bitcast(I32), ACT.Square,
                                                        bias=subcol[:, n:n + 1], scale=BIG)
                        last.then_inc(token_scalar_vector.handle, 1)
                        ac.wait_ge(token_tensor_scalar.handle, 1)
                        ac.sem_clear(token_tensor_scalar.handle)
                        nc.scalar.activation(res[:], dif[:], ACT.Exp)
                        nc.scalar.activation(avm[:], bank[6][0:WIN, 64:64 + 2 * H], ACT.Copy).then_inc(token_scalar_tensor.handle, 1)
                        ac.wait_ge(token_vector_scalar.handle, 1)
                        ac.sem_clear(token_vector_scalar.handle)
                        nc.scalar.activation(msg[0][:, :, D:ROW], z[:], ACT.Exp).then_inc(token_scalar_vector.handle, 1)
                    further(ac, group, window)

                @block.vector
                def _(ve):
                    nc.vector.memset(shift[:], 0.0).then_inc(f_done.handle, 1)

                    def group(g):
                        ve.wait_ge(f_load.handle, (g + 1) * 32)
                        ve.wait_ge(f_scores.handle, g + 1)
                        settle(ve, nc.vector.memset(shift[:], 0.0))

                    def window(g, k, start):
                        settle(ve, next_window(ve, g))
                        settle(ve, nc.vector.tensor_tensor(base_col[:], first[:, ds(g, 1)], shift[:], ALU.add))
                        settle(ve, nc.vector.tensor_tensor(stcol[:], part[:], base_col[:], ALU.add))
                        settle(ve, nc.vector.tensor_scalar(bufB[0][0:WIN, :], bufA[0][0:WIN, :].bitcast(I32), stcol[0:WIN, :],
                                                           None, ALU.is_equal))
                        nc.vector.tensor_scalar(subcol[:], subnode[:], base_col[:], -BIG, ALU.add, ALU.mult).then_inc(token_vector_scalar.handle, 1)
                        ve.wait_ge(token_scalar_vector.handle, 1)
                        ve.sem_clear(token_scalar_vector.handle)
                        for n in range(NSUB):
                            for h in range(2):
                                last = nc.vector.tensor_tensor_reduce(
                                    out=far[n][:, h * 512:(h + 1) * 512], in0=bank[2 + h][:],
                                    in1=far[n][:, h * 512:(h + 1) * 512], scale=1.0, scalar=-3.0e38, op0=ALU.subtract,
                                    op1=ALU.max, accum_out=submax2[:, n, h:h + 1])
                        settle(ve, last)
                        settle(ve, nc.vector.tensor_reduce(submax[:], submax2[:], AX, ALU.max))
                        nc.vector.tensor_tensor(subpick[:], bc(submax[:], [P, NSUB, SUB], 2),
                                                     bc(pick[:], [P, NSUB, SUB], 1), ALU.mult).then_inc(token_vector_tensor.handle, 1)
                        ve.wait_ge(token_tensor_vector.handle, 1)
                        ve.sem_clear(token_tensor_vector.handle)
                        start = nc.s_assert_within(start, 0, N, skip_runtime_bounds_check_because="a window starts at or below the last destination")
                        m = xT[0:H, ds(start, WIN)]
                        a = auxT[0:H, ds(start, WIN)]
                        nc.vector.tensor_copy(adw[:], a)
                        settle(ve, nc.vector.tensor_tensor(U[:, 0, :], m, a, ALU.add))
                        settle(ve, nc.vector.tensor_tensor(m, m, bank[6][0:H, 0:WIN], ALU.max))
                        settle(ve, nc.vector.tensor_tensor(U[:, 1, :], m, a, ALU.add))
                        settle(ve, nc.vector.scalar_tensor_tensor(V[:], U[:], SLOPE, U[:], ALU.mult, ALU.max))
                        nc.vector.tensor_tensor(dif[:], V[:, 0, :], V[:, 1, :], ALU.subtract).then_inc(token_vector_tensor.handle, 1)
                        ve.wait_ge(token_tensor_vector.handle, 1)
                        ve.sem_clear(token_tensor_vector.handle)
                        ed = bank[4][:, 0:G * 2 * H].rearrange("p (j v) -> p j v", v=2 * H)
                        settle(ve, nc.vector.tensor_tensor(z[:], rows[0][:, :, D:ROW], ed[:, :, 0:H], ALU.add))
                        settle(ve, nc.vector.scalar_tensor_tensor(z[:], z[:], SLOPE, z[:], ALU.mult, ALU.max))
                        settle(ve, nc.vector.tensor_tensor(z[:], z[:], ed[:, :, H:2 * H], ALU.subtract))
                        nc.vector.tensor_scalar(z[:], z[:], 0.0, None, ALU.min).then_inc(token_vector_scalar.handle, 1)
                        ve.wait_ge(token_scalar_vector.handle, 1)
                        ve.sem_clear(token_scalar_vector.handle)
                        nc.vector.tensor_tensor(msg[0][:, :, 0:D].rearrange("p j (h c) -> p j h c", c=C),
                                                     rows[0][:, :, 0:D].rearrange("p j (h c) -> p j h c", c=C),
                                                     bc(msg[0][:, :, D:ROW], [P, G, H, C], 3), ALU.mult).then_inc(token_vector_tensor.handle, 1)
                        ve.wait_ge(token_tensor_vector.handle, 1)
                        ve.sem_clear(token_tensor_vector.handle)
                        w = accT[0:ROW, ds(start, WIN)]
                        settle(ve, nc.vector.tensor_tensor(w, w, bank[5][0:ROW, 64:64 + WIN], ALU.mult))
                        settle(ve, nc.vector.tensor_tensor(w, w, bank[5][0:ROW, 0:WIN], ALU.add))

                    def closing(g):
                        nc.vector.memset(base_col[:], 0.0).then_inc(f_done.handle, 1)
                    further(ve, group, window, closing)

        def sum_pass(name, table, attr=False, aux=False):
            s_rows = [sem(f"{name}_rows_loaded{i}") for i in range(R)]
            with nc.Block() as block:
                @block.sync
                def _(sp):
                    def body(g, s, it):
                        if due(it * 16 * G):
                            sp.wait_ge(s_rows[s].handle, s_rows[s].at(it * 16 * G))
                        sp.dma_start(idx[s][:], A["src"][ds(g, 1), :, :].rearrange("o p j -> (o p) j")
                                     ).then_inc(s_idx[s].handle, 16)
                        if attr:
                            if due(g - R + 1):
                                sp.wait_ge(q["ea_ready"].handle, q["ea_ready"].at(g - R + 1))
                            sp.dma_start(bufB[s][0:EA, :], A["attr16"][ds(g, 1), :, :].rearrange("o k e -> (o k) e")
                                         ).then_inc(s_bB[s].handle, 16)
                        if aux:
                            if due(g - R + 1):
                                sp.wait_ge(q["aux_ready"].handle, q["aux_ready"].at(g - R + 1))
                            sp.dma_start(bufA[s][:].rearrange("p (j d) -> p j d", d=P)[:, :, D:P],
                                         A["attr64"][ds(g, 1), :, :].rearrange("o p (j d) -> (o p) j d", d=D)
                                         ).then_inc(s_bA[s].handle, 16)
                    turns(body)(sp.Fori)

                @block.gpsimd
                def _(po):
                    def body(g, s, it):
                        po.wait_ge(s_idx[s].handle, s_idx[s].at(it * 16 + 16))
                        if due(g - R + 1):
                            po.wait_ge(q["rows_free" if attr else "msg_ready"].handle, q["rows_free" if attr else "msg_ready"].at(g - R + 1))
                        po.sem_inc(s_passed.handle, 1)
                        for j in range(G):
                            nc.gpsimd.indirect_dma_start(rows[s][:, j, 0:D], None, table,
                                                         bass.IndirectOffsetOnAxis(idx[s][:, j:j + 1], 0)
                                                         ).then_inc(s_rows[s].handle, 16)
                    turns(body)(po.Fori)

                @block.tensor
                def _(pe):
                    def body(g, s, it):
                        if attr:
                            pe.wait_ge(s_bB[s].handle, s_bB[s].at(it * 16 + 16))
                            if due(g - R + 1):
                                pe.wait_ge(q["rows_free"].handle, q["rows_free"].at(g - R + 1))
                            for j in range(G):
                                last = nc.tensor.matmul(bank[s][:, j * D:(j + 1) * D],
                                                        bufB[s][0:EA, j * P:(j + 1) * P], emb[:], start=True, stop=True)
                            last.then_inc(q["ea_ready"].handle, 1)
                        pe.wait_ge(q["sel_ready"].handle, q["sel_ready"].at(g + 1))
                        if aux:
                            pe.wait_ge(s_bA[s].handle, s_bA[s].at(it * 16 + 16))
                            if due(g):
                                pe.wait_ge(q["auxacc_done"].handle, q["auxacc_done"].at(g))
                            for j in range(G):
                                last = nc.tensor.matmul(bank[6][:, 0:WIN], bufA[s][:, j * P:(j + 1) * P], sel[s][:, j, :],
                                                        start=j == 0, stop=j == G - 1)
                            last.then_inc(q["aux_ready"].handle, 1)
                        pe.wait_ge(q["msg_ready"].handle, q["msg_ready"].at(g + 1))
                        if due(g - R + 1):
                            pe.wait_ge(q["acc_done"].handle, q["acc_done"].at(g - R + 1))
                        for j in range(G):
                            last = nc.tensor.matmul(bank[3 + s][0:D, 0:WIN], msg[s][:, j, 0:D], sel[s][:, j, :],
                                                    start=j == 0, stop=j == G - 1)
                        last.then_inc(q["sum_ready"].handle, 1)
                    turns(body)(pe.Fori)

                @block.vector
                def _(ve):
                    def add_sums(g, s):
                        base = ve.value_load(first_i[0:1, ds(g, 1)], min_val=0, max_val=N)
                        w = accT[0:D, ds(base, WIN)]
                        ve.wait_ge(q["sum_ready"].handle, q["sum_ready"].at(g + 1))
                        if due(g):
                            ve.wait_ge(q["acc_done"].handle, q["acc_done"].at(g))
                        nc.vector.tensor_tensor(w, w, bank[3 + s][0:D, 0:WIN], ALU.add).then_inc(q["acc_done"].handle, 1)
                        if aux:
                            if due(g):
                                ve.wait_ge(q["auxacc_done"].handle, q["auxacc_done"].at(g))
                            w = auxT[:, ds(base, WIN)]
                            nc.vector.tensor_tensor(w, w, bank[6][:, 0:WIN], ALU.add).then_inc(q["auxacc_done"].handle, 1)

                    def body(g, s, it):
                        if due(g - R + 1):
                            ve.wait_ge(q["sum_ready"].handle, q["sum_ready"].at(g - R + 1))
                        nc.vector.tensor_tensor(sel[s][:], bc(iota[:], [P, G, WIN], 1), bc(drel[:, ds(g, 1), :].rearrange("p o j -> p (o j)"), [P, G, WIN], 2),
                                                ALU.is_equal).then_inc(q["sel_ready"].handle, 1)
                        if not (isinstance(g, int) and g == 0):
                            add_sums(g - 1, (s - 1) % R)
                        ve.wait_ge(s_rows[s].handle, s_rows[s].at((it + 1) * 16 * G))
                        if attr:
                            ve.wait_ge(q["ea_ready"].handle, q["ea_ready"].at(g + 1))
                            if due(g - R + 1):
                                ve.wait_ge(q["msg_ready"].handle, q["msg_ready"].at(g - R + 1))
                            nc.vector.tensor_tensor(far[s][:, 0:G * D].rearrange("p (j d) -> p j d", d=D), rows[s][:, :, 0:D],
                                                    bank[s][:].rearrange("p (j d) -> p j d", d=D), ALU.add
                                                    ).then_inc(q["rows_free"].handle, 1)
                        else:
                            nc.vector.tensor_tensor(msg[s][:, :, 0:D], rows[s][:, :, 0:D],
                                                    bc(wgt[:, ds(g, 1), :].rearrange("p o j -> p (o j)"), [P, G, D], 2), ALU.mult
                                                    ).then_inc(q["msg_ready"].handle, 1)
                    turns(body)(ve.Fori)
                    add_sums(NG - 1, (NG - 1) % R)

                if attr:
                    @block.scalar
                    def _(ac):
                        def body(g, s, it):
                            ac.wait_ge(q["rows_free"].handle, q["rows_free"].at(g + 1))
                            if due(g - R + 1):
                                ac.wait_ge(q["sum_ready"].handle, q["sum_ready"].at(g - R + 1))
                            nc.scalar.activation(msg[s][:, :, 0:D], far[s][:, 0:G * D].rearrange("p (j d) -> p j d", d=D),
                                                 ACT.Relu).then_inc(q["msg_ready"].handle, 1)
                        turns(body)(ac.Fori)
            for s in range(R):
                s_idx[s].done(16 * slot_total(s))
                if attr:
                    s_bB[s].done(16 * slot_total(s))
                if aux:
                    s_bA[s].done(16 * slot_total(s))
            for n in ["sel_ready", "msg_ready", "acc_done", "sum_ready"] + ["ea_ready", "rows_free"] * attr + ["aux_ready", "auxacc_done"] * aux:
                q[n].done(NG)
            sum_further(name, table, attr, aux)

        def chunks(fori, body, link=None):
            body(0)
            if link is not None:
                link.per = link.close()
            with fori(1, NCH) as c:
                if link is not None:
                    link.offset = c * link.per
                body(c)
            if link is not None:
                assert link.close() == link.per
                link.sem.total = link.per * NCH

        LO = slice(0, D)

        def chunk(table, part_rows, c):
            return table[part_rows, ds(c * CH, CH)]

        def tiles(c):
            return X[:, ds(c * TC, TC), :]

        def table_rows(table, c):
            return table[ds(c * CH, CH), :].rearrange("(t p) d -> p t d", p=P)

        def by_tile(b, width=D):
            return b[:, 0:TC * width].rearrange("p (t d) -> p t d", d=width)

        def to_nodes(b, src, rhs, width):
            for t in range(TC):
                last = nc.tensor.matmul(b[:, t * width:(t + 1) * width], src[:, t * P:(t + 1) * P], rhs,
                                        start=True, stop=True)
            return last

        def layer_norm(ve, link, y, o, n):
            link(nc.vector.tensor_reduce(st[:, 0, :], y[:], AX, ALU.add))
            link(nc.vector.tensor_scalar(st[:, 0, :], st[:, 0, :], 1.0 / D, None, ALU.mult))
            link(nc.vector.tensor_tensor(y[:], y[:], bc(st[:, 0, :], [P, TC, D], 2), ALU.subtract))
            link(nc.vector.tensor_tensor(qbuf[:], y[:], y[:], ALU.mult))
            link(nc.vector.tensor_reduce(st[:, 1, :], qbuf[:], AX, ALU.add))
            nc.vector.tensor_scalar(st[:, 1, :], st[:, 1, :], 1.0 / D, EPS, ALU.mult, ALU.add
                                    ).then_inc(q["root_asked"].handle, 1)
            ve.wait_ge(q["root_done"].handle, q["root_done"].at(n))
            link(nc.vector.reciprocal(st[:, 3, :], st[:, 2, :]))
            return nc.vector.tensor_tensor(o[:], y[:], bc(st[:, 3, :], [P, TC, D], 2), ALU.mult)

        def root(ac, n):
            ac.wait_ge(q["root_asked"].handle, q["root_asked"].at(n))
            nc.scalar.activation(st[:, 2, :], st[:, 1, :], ACT.Sqrt).then_inc(q["root_done"].handle, 1)

        def sage_dense(i):
            last_one = i == 2
            with nc.Block() as block:
                @block.vector
                def _(ve):
                    link = Chain(ve, s_ve)
                    if i == 0:
                        cnt = auxT[LO, :]
                        nc.vector.tensor_scalar(cnt, cnt, 1.0, None, ALU.max).then_inc(q["once"].handle, 1)
                        ve.wait_ge(q["once"].handle, q["once"].at(1))
                        nc.vector.reciprocal(cnt, cnt).then_inc(q["once"].handle, 1)
                        ve.wait_ge(q["once"].handle, q["once"].at(2))

                    def body(c):
                        if due(c):
                            ve.wait_ge(q["prod_ready"].handle, q["prod_ready"].at(c))
                        nc.vector.tensor_tensor(abuf[LO, :], chunk(accT, LO, c), chunk(auxT, LO, c), ALU.mult
                                                ).then_inc(q["mean_ready"].handle, 1)
                        ve.wait_ge(q["mean_ready"].handle, q["mean_ready"].at(c + 1))
                        ve.sem_inc(s_passed.handle, 1)
                        nc.vector.tensor_copy(chunk(accT, LO, c), zeros[LO, :]).then_inc(q["cleared"].handle, 1)
                        ve.wait_ge(q["nodes_ready"].handle, q["nodes_ready"].at(c + 1))
                        if due(16 * c):
                            ve.wait_ge(s_tab.handle, s_tab.at(16 * c))
                        if last_one:
                            link(nc.vector.tensor_tensor(ybuf[:], by_tile(bank[1]), tiles(c), ALU.add))
                            link(layer_norm(ve, link, ybuf, tbuf, c + 1))
                            ve.sem_inc(s_passed.handle, 1)
                            nc.vector.tensor_copy(tiles(c), tbuf[:]).then_inc(q["tile_ready"].handle, 1)
                        else:
                            nc.vector.tensor_copy(tbuf[:], by_tile(bank[1])).then_inc(q["tile_ready"].handle, 1)
                    chunks(ve.Fori, body, link)

                @block.tensor
                def _(pe):
                    def body(c):
                        pe.wait_ge(q["mean_ready"].handle, q["mean_ready"].at(c + 1))
                        pe.wait_ge(q["x_ready"].handle, q["x_ready"].at(c + 1))
                        if due(c):
                            pe.wait_ge(q["act_ready"].handle, q["act_ready"].at(c))
                        pe.sem_inc(s_passed.handle, 1)
                        nc.tensor.matmul(bank[0][LO, :], wm[f"Wl{i}"][:], abuf[LO, :], start=True, stop=False)
                        nc.tensor.matmul(bank[0][LO, :], wm[f"Wr{i}"][:], xbuf[:], start=False, stop=True
                                         ).then_inc(q["prod_ready"].handle, 1)
                        pe.wait_ge(q["act_ready"].handle, q["act_ready"].at(c + 1))
                        if due(c):
                            pe.wait_ge(q["tile_ready"].handle, q["tile_ready"].at(c))
                        pe.sem_inc(s_passed.handle, 1)
                        to_nodes(bank[1], hbuf, ident[LO, LO], D).then_inc(q["nodes_ready"].handle, 1)
                    chunks(pe.Fori, body)

                @block.scalar
                def _(ac):
                    def body(c):
                        if due(c):
                            ac.wait_ge(q["prod_ready"].handle, q["prod_ready"].at(c))
                        nc.scalar.activation(xbuf[:], chunk(xT, LO, c), ACT.Copy).then_inc(q["x_ready"].handle, 1)
                        ac.wait_ge(q["prod_ready"].handle, q["prod_ready"].at(c + 1))
                        if due(c):
                            ac.wait_ge(q["nodes_ready"].handle, q["nodes_ready"].at(c))
                        nc.scalar.activation(hbuf[:], bank[0][LO, :], ACT.Identity if last_one else ACT.Relu,
                                             bias=col[f"bl{i}"]).then_inc(q["act_ready"].handle, 1)
                        if last_one:
                            root(ac, c + 1)
                        else:
                            ac.wait_ge(q["act_ready"].handle, q["act_ready"].at(c + 1))
                            ac.sem_inc(s_passed.handle, 1)
                            nc.scalar.activation(chunk(xT, LO, c), hbuf[:], ACT.Copy).then_inc(q["kept"].handle, 1)
                    chunks(ac.Fori, body)

                @block.sync
                def _(sp):
                    def body(c):
                        sp.wait_ge(q["tile_ready"].handle, q["tile_ready"].at(c + 1))
                        sp.dma_start(table_rows(node_table, c), tbuf[:]).then_inc(s_tab.handle, 16)
                    chunks(sp.Fori, body)
                    sp.wait_ge(s_tab.handle, s_tab.at(16 * NCH))
            s_ve.done(s_ve.total)
            s_tab.done(16 * NCH)
            q["once"].done(2 * (i == 0))
            for n in ["prod_ready", "mean_ready", "cleared", "nodes_ready", "tile_ready", "x_ready", "act_ready"]:
                q[n].done(NCH)
            for n in ["root_asked", "root_done"] if last_one else ["kept"]:
                q[n].done(NCH)

        def gin_dense0():
            with nc.Block() as block:
                @block.vector
                def _(ve):
                    def body(c):
                        if due(c):
                            ve.wait_ge(q["prod_ready"].handle, q["prod_ready"].at(c))
                        nc.vector.tensor_copy(abuf[LO, :], chunk(accT, LO, c)).then_inc(q["mean_ready"].handle, 1)
                        ve.wait_ge(q["mean_ready"].handle, q["mean_ready"].at(c + 1))
                        ve.sem_inc(s_passed.handle, 1)
                        nc.vector.tensor_copy(chunk(accT, LO, c), zeros[LO, :]).then_inc(q["cleared"].handle, 1)
                        ve.wait_ge(q["nodes_ready"].handle, q["nodes_ready"].at(c + 1))
                        if due(16 * c):
                            ve.wait_ge(s_tab.handle, s_tab.at(16 * c))
                        nc.vector.tensor_copy(tbuf[:], by_tile(bank[1])).then_inc(q["tile_ready"].handle, 1)
                    chunks(ve.Fori, body)

                @block.tensor
                def _(pe):
                    def body(c):
                        pe.wait_ge(q["mean_ready"].handle, q["mean_ready"].at(c + 1))
                        if due(c):
                            pe.wait_ge(q["act_ready"].handle, q["act_ready"].at(c))
                        pe.sem_inc(s_passed.handle, 1)
                        nc.tensor.matmul(bank[0][LO, :], wm["W10"][:], abuf[LO, :], start=True, stop=True
                                         ).then_inc(q["prod_ready"].handle, 1)
                        pe.wait_ge(q["act_ready"].handle, q["act_ready"].at(c + 1))
                        if due(c):
                            pe.wait_ge(q["tile_ready"].handle, q["tile_ready"].at(c))
                        to_nodes(bank[1], hbuf, wm["W20"][:], D).then_inc(q["nodes_ready"].handle, 1)
                    chunks(pe.Fori, body)

                @block.scalar
                def _(ac):
                    def body(c):
                        ac.wait_ge(q["prod_ready"].handle, q["prod_ready"].at(c + 1))
                        if due(c):
                            ac.wait_ge(q["nodes_ready"].handle, q["nodes_ready"].at(c))
                        nc.scalar.activation(hbuf[:], bank[0][LO, :], ACT.Relu).then_inc(q["act_ready"].handle, 1)
                    chunks(ac.Fori, body)

                @block.sync
                def _(sp):
                    def body(c):
                        sp.wait_ge(q["tile_ready"].handle, q["tile_ready"].at(c + 1))
                        sp.dma_start(table_rows(node_table, c), tbuf[:]).then_inc(s_tab.handle, 16)
                    chunks(sp.Fori, body)
                    sp.wait_ge(s_tab.handle, s_tab.at(16 * NCH))
            s_tab.done(16 * NCH)
            for n in ["prod_ready", "mean_ready", "cleared", "nodes_ready", "tile_ready", "act_ready"]:
                q[n].done(NCH)

        def attend_pe(pe, k, c):
            pe.wait_ge(q["x_ready"].handle, q["x_ready"].at(c + 1))
            if due(c):
                pe.wait_ge(q["h_ready"].handle, q["h_ready"].at(c))
            pe.sem_inc(s_passed.handle, 1)
            nc.tensor.matmul(bank[4][LO, :], wm["G" + k][:], xbuf[:], start=True, stop=True
                             ).then_inc(q["hprod_ready"].handle, 1)
            pe.wait_ge(q["h_ready"].handle, q["h_ready"].at(c + 1))
            if due(c):
                pe.wait_ge(q["gtile_ready"].handle, q["gtile_ready"].at(c))
            pe.sem_inc(s_passed.handle, 1)
            nc.tensor.matmul(bank[5][0:H, :], rowsel[k][:, D:ROW], hbuf[:], start=True, stop=True)
            nc.tensor.matmul(bank[6][0:H, :], adsel[k][:], hbuf[:], start=True, stop=True)
            to_nodes(bank[7], hbuf, rowsel[k][:], ROW).then_inc(q["scored"].handle, 1)

        def attend_act(ac, c):
            ac.wait_ge(q["hprod_ready"].handle, q["hprod_ready"].at(c + 1))
            if due(c):
                ac.wait_ge(q["gtile_ready"].handle, q["gtile_ready"].at(c))
            nc.scalar.activation(hbuf[:], bank[4][LO, :], ACT.Copy).then_inc(q["h_ready"].handle, 1)

        def attend_ve(ve, c):
            ve.wait_ge(q["scored"].handle, q["scored"].at(c + 1))
            if due(16 * c):
                ve.wait_ge(s_tab.handle, s_tab.at(16 * c))
            ve.sem_inc(s_passed.handle, 1)
            nc.vector.tensor_copy(chunk(xT, slice(0, H), c), bank[5][0:H, :])
            nc.vector.tensor_copy(chunk(auxT, slice(0, H), c), bank[6][0:H, :])
            nc.vector.tensor_copy(chunk(accT, LO, c), hbuf[:])
            nc.vector.tensor_copy(chunk(accT, slice(D, ROW), c), ones[:])
            nc.vector.tensor_copy(gbuf[:], by_tile(bank[7], ROW)).then_inc(q["gtile_ready"].handle, 1)

        def attend_sp(sp):
            def body(c):
                sp.wait_ge(q["gtile_ready"].handle, q["gtile_ready"].at(c + 1))
                sp.dma_start(table_rows(gat_table, c), gbuf[:]).then_inc(s_tab.handle, 16)
            chunks(sp.Fori, body)
            sp.wait_ge(s_tab.handle, s_tab.at(16 * NCH))

        attend_sems = ["x_ready", "h_ready", "hprod_ready", "scored", "gtile_ready"]

        def gin_dense1():
            with nc.Block() as block:
                @block.vector
                def _(ve):
                    link = Chain(ve, s_ve)

                    def body(c):
                        nc.vector.tensor_copy(abuf[LO, :], chunk(accT, LO, c))
                        nc.vector.tensor_copy(abuf[D:P, :], chunk(auxT, slice(D, P), c)).then_inc(q["mean_ready"].handle, 1)
                        ve.wait_ge(q["nodes_ready"].handle, q["nodes_ready"].at(c + 1))
                        link(nc.vector.tensor_copy(ybuf[:], by_tile(bank[1])))
                        link(nc.vector.tensor_tensor(qbuf[:], ybuf[:], ybuf[:], ALU.mult))
                        nc.vector.tensor_reduce(st[:, 1, :], qbuf[:], AX, ALU.add).then_inc(q["root_asked"].handle, 1)
                        ve.wait_ge(q["root_done"].handle, q["root_done"].at(3 * c + 1))
                        link(nc.vector.tensor_scalar(st[:, 2, :], st[:, 2, :], 1e-12, None, ALU.max))
                        link(nc.vector.reciprocal(st[:, 3, :], st[:, 2, :]))
                        link(nc.vector.tensor_tensor(ybuf[:], ybuf[:], bc(st[:, 3, :], [P, TC, D], 2), ALU.mult))
                        link(nc.vector.tensor_tensor(ybuf[:], ybuf[:], tiles(c), ALU.add))
                        link(layer_norm(ve, link, ybuf, tbuf, 3 * c + 2))
                        link(nc.vector.tensor_tensor(ybuf[:], tbuf[:], by_tile(bank[2]), ALU.mult))
                        link(nc.vector.tensor_tensor(ybuf[:], ybuf[:], tbuf[:], ALU.add))
                        nxt = layer_norm(ve, link, ybuf, tbuf, 3 * c + 3)
                        nxt.then_inc(q["tile_ready"].handle, 1)
                        ve.wait_ge(q["tile_ready"].handle, q["tile_ready"].at(c + 1))
                        ve.sem_inc(s_passed.handle, 1)
                        link.mark(nc.vector.tensor_copy(tiles(c), tbuf[:]))
                        attend_ve(ve, c)
                        ve.wait_ge(q["gtile_ready"].handle, q["gtile_ready"].at(c + 1))
                    chunks(ve.Fori, body, link)

                @block.tensor
                def _(pe):
                    def body(c):
                        pe.wait_ge(q["mean_ready"].handle, q["mean_ready"].at(c + 1))
                        pe.sem_inc(s_passed.handle, 1)
                        nc.tensor.matmul(bank[0][LO, :], wm["W11"][:], abuf[LO, :], start=True, stop=True
                                         ).then_inc(q["prod_ready"].handle, 1)
                        to_nodes(bank[2], abuf[D:P, :], ident[D:P, D:P], D)
                        pe.wait_ge(q["act_ready"].handle, q["act_ready"].at(c + 1))
                        to_nodes(bank[1], hbuf, wm["W21"][:], D).then_inc(q["nodes_ready"].handle, 1)
                        pe.wait_ge(q["tile_ready"].handle, q["tile_ready"].at(c + 1))
                        for t in range(TC):
                            last = nc.tensor.matmul(bank[3][LO, t * P:(t + 1) * P], tbuf[:, t, :], ident[:],
                                                    start=True, stop=True)
                        last.then_inc(q["back_ready"].handle, 1)
                        attend_pe(pe, "1", c)
                    chunks(pe.Fori, body)

                @block.scalar
                def _(ac):
                    def body(c):
                        ac.wait_ge(q["prod_ready"].handle, q["prod_ready"].at(c + 1))
                        nc.scalar.activation(hbuf[:], bank[0][LO, :], ACT.Relu).then_inc(q["act_ready"].handle, 1)
                        root(ac, 3 * c + 1)
                        root(ac, 3 * c + 2)
                        root(ac, 3 * c + 3)
                        ac.wait_ge(q["back_ready"].handle, q["back_ready"].at(c + 1))
                        nc.scalar.activation(xbuf[:], bank[3][LO, :], ACT.Copy).then_inc(q["x_ready"].handle, 1)
                        attend_act(ac, c)
                    chunks(ac.Fori, body)

                @block.sync
                def _(sp):
                    attend_sp(sp)
            s_ve.done(s_ve.total)
            s_tab.done(16 * NCH)
            for n in attend_sems + ["prod_ready", "mean_ready", "nodes_ready", "tile_ready", "act_ready", "back_ready"]:
                q[n].done(NCH)
            for n in ["root_asked", "root_done"]:
                q[n].done(3 * NCH)

        def gat_dense(k, nxt):
            bias = col["gb" + k]
            with nc.Block() as block:
                @block.vector
                def _(ve):
                    link = Chain(ve, s_ve)

                    def body(c):
                        ve.wait_ge(q["prod_ready"].handle, q["prod_ready"].at(c + 1))
                        link(nc.vector.reciprocal(abuf[LO, :], bank[0][LO, :]))
                        nc.vector.tensor_tensor(abuf[LO, :], abuf[LO, :], chunk(accT, LO, c), ALU.mult
                                                ).then_inc(q["mean_ready"].handle, 1)
                        if nxt:
                            attend_ve(ve, c)
                            ve.wait_ge(q["gtile_ready"].handle, q["gtile_ready"].at(c + 1))
                        else:
                            ve.wait_ge(q["nodes_ready"].handle, q["nodes_ready"].at(c + 1))
                            if due(16 * c):
                                ve.wait_ge(s_tab.handle, s_tab.at(16 * c))
                            link(nc.vector.tensor_tensor(ybuf[:], by_tile(bank[1]), tiles(c), ALU.add))
                            layer_norm(ve, link, ybuf, tbuf, c + 1).then_inc(q["tile_ready"].handle, 1)
                            ve.wait_ge(q["tile_ready"].handle, q["tile_ready"].at(c + 1))
                    chunks(ve.Fori, body, link)

                @block.tensor
                def _(pe):
                    def body(c):
                        if due(c):
                            pe.wait_ge(q["gtile_ready" if nxt else "tile_ready"].handle, q["gtile_ready" if nxt else "tile_ready"].at(c))
                        nc.tensor.matmul(bank[0][LO, :], denom[:], chunk(accT, slice(0, ROW), c), start=True, stop=True
                                         ).then_inc(q["prod_ready"].handle, 1)
                        if nxt:
                            attend_pe(pe, nxt, c)
                        else:
                            pe.wait_ge(q["x_ready"].handle, q["x_ready"].at(c + 1))
                            to_nodes(bank[1], xbuf, ident[LO, LO], D).then_inc(q["nodes_ready"].handle, 1)
                    chunks(pe.Fori, body)

                @block.scalar
                def _(ac):
                    def body(c):
                        ac.wait_ge(q["mean_ready"].handle, q["mean_ready"].at(c + 1))
                        nc.scalar.activation(xbuf[:], abuf[LO, :], ACT.Relu if nxt else ACT.Identity, bias=bias
                                             ).then_inc(q["x_ready"].handle, 1)
                        if nxt:
                            attend_act(ac, c)
                        else:
                            root(ac, c + 1)
                    chunks(ac.Fori, body)

                @block.sync
                def _(sp):
                    if nxt:
                        attend_sp(sp)
                    else:
                        full = N // CH
                        with sp.Fori(0, full) as c:
                            sp.wait_ge(q["tile_ready"].handle, q["tile_ready"].at(c + 1))
                            sp.dma_start(table_rows(out, c), tbuf[:]).then_inc(s_tab.handle, 16)
                        sp.wait_ge(q["tile_ready"].handle, q["tile_ready"].at(NCH))
                        left, t, n = N - full * CH, 0, 0
                        while left > 0:
                            r = min(left, P)
                            sp.dma_start(out[full * CH + t * P:full * CH + t * P + r, :], tbuf[0:r, t, :]
                                         ).then_inc(s_tab.handle, 16)
                            left, t, n = left - r, t + 1, n + 1
                        sp.wait_ge(s_tab.handle, s_tab.at(16 * (full + n)))
            s_ve.done(s_ve.total)
            s_tab.done(16 * NCH)
            for n in ["prod_ready", "mean_ready"] + (attend_sems if nxt else ["x_ready", "nodes_ready", "tile_ready", "root_asked", "root_done"]):
                q[n].done(NCH)

        def gat_pass(name):
            s_rows = [sem(f"{name}_rows_loaded{i}") for i in range(RG)]
            edge = bank[4]
            wide = [bank[5], bank[7]]
            small = bank[6]

            def has(g, before):
                return not isinstance(g, int) or g >= before

            def following(g, s, it):
                return g + 1, (s + 1) % RG, it + (s + 1) // RG

            with nc.Block() as block:
                @block.sync
                def _(sp):
                    def body(g, s, it):
                        if due(it * 16 * G):
                            sp.wait_ge(s_rows[s].handle, s_rows[s].at(it * 16 * G))
                        sp.dma_start(idx[s][:], A["src"][ds(g, 1), :, :].rearrange("o p j -> (o p) j")
                                     ).then_inc(s_idx[s].handle, 16)
                        if due(g - RG + 1):
                            sp.wait_ge(q["selT_ready"].handle, q["selT_ready"].at(g - RG + 1))
                        sp.dma_start(bufA[s][:].bitcast(I32), A["dst_rows"][ds(g, 1), :].broadcast_to([P, GE])
                                     ).then_inc(s_bA[s].handle, 16)
                    turns(body, RG)(sp.Fori)

                @block.gpsimd
                def _(po):
                    def body(g, s, it):
                        po.wait_ge(s_idx[s].handle, s_idx[s].at(it * 16 + 16))
                        if due(g - RG + 1):
                            po.wait_ge(q["msg_ready"].handle, q["msg_ready"].at(g - RG + 1))
                        po.sem_inc(s_passed.handle, 1)
                        for j in range(G):
                            nc.gpsimd.indirect_dma_start(rows[s][:, j, :], None, gat_table,
                                                         bass.IndirectOffsetOnAxis(idx[s][:, j:j + 1], 0)
                                                         ).then_inc(s_rows[s].handle, 16)
                    turns(body, RG)(po.Fori)

                @block.tensor
                def _(pe):
                    def shifts(g):
                        pe.wait_ge(q["shift_ready"].handle, q["shift_ready"].at(g + 1))
                        if due(g):
                            pe.wait_ge(q["avm_ready"].handle, q["avm_ready"].at(g))
                        nc.tensor.matmul(small[0:WIN, 64:64 + H], adw[:], ident[0:H, 0:H], start=True, stop=True)
                        nc.tensor.matmul(small[0:WIN, 64 + H:64 + 2 * H], V[:, 1, :], ident[0:H, 0:H],
                                         start=True, stop=True).then_inc(q["colsT_ready"].handle, 1)

                    def factors(g, s):
                        pe.wait_ge(q["res_ready"].handle, q["res_ready"].at(g + 1))
                        if due(g - 1):
                            pe.wait_ge(q["acc_done"].handle, q["acc_done"].at(g - 1))
                        nc.tensor.matmul(wide[s % 2][0:ROW, 64:64 + WIN], widen[:], res[:], start=True, stop=True
                                         ).then_inc(q["wide_ready"].handle, 1)

                    def values(g, s):
                        pe.wait_ge(q["avm_ready"].handle, q["avm_ready"].at(g + 1))
                        pe.wait_ge(q["selT_ready"].handle, q["selT_ready"].at(g + 1))
                        if due(g):
                            pe.wait_ge(q["z_done"].handle, q["z_done"].at(g))
                        for j in range(G):
                            last = nc.tensor.matmul(edge[:, j * 2 * H:(j + 1) * 2 * H], bufB[s][0:WIN, j * P:(j + 1) * P],
                                                    avm[:], start=True, stop=True)
                        last.then_inc(q["edge_ready"].handle, 1)

                    def sums(g, s):
                        pe.wait_ge(q["sel_ready"].handle, q["sel_ready"].at(g + 1))
                        pe.wait_ge(q["msg_ready"].handle, q["msg_ready"].at(g + 1))
                        for j in range(G):
                            last = nc.tensor.matmul(wide[s % 2][0:ROW, 0:WIN], msg[s][:, j, :], sel[s][:, j, :],
                                                    start=j == 0, stop=j == G - 1)
                        last.then_inc(q["sum_ready"].handle, 1)

                    def body(g, s, it):
                        pe.wait_ge(q["rep_ready"].handle, q["rep_ready"].at(g + 1))
                        if due(NSUB * g):
                            pe.wait_ge(q["max_done"].handle, q["max_done"].at(NSUB * g))
                        for j in range(G):
                            last = nc.tensor.transpose(scores[:, j * P:(j + 1) * P], rep[:, j, :], ident[:])
                        last.then_inc(q["scores_ready"].handle, 1)
                        if has(g, 1):
                            shifts(g - 1)
                            factors(g - 1, (s - 1) % RG)
                            values(g - 1, (s - 1) % RG)
                        if has(g, 2):
                            sums(g - 2, (s - 2) % RG)
                        pe.wait_ge(q["pick_ready"].handle, q["pick_ready"].at(g + 1))
                        nc.tensor.matmul(small[0:H, 0:WIN], heads[:], subpick[:].rearrange("p a b -> p (a b)"),
                                         start=True, stop=True).then_inc(q["winmax_ready"].handle, 1)
                    turns(body, RG)(pe.Fori)
                    sums(NG - 2, (NG - 2) % RG)
                    shifts(NG - 1)
                    factors(NG - 1, (NG - 1) % RG)
                    values(NG - 1, (NG - 1) % RG)
                    sums(NG - 1, (NG - 1) % RG)

                @block.scalar
                def _(ac):
                    def columns(g):
                        ac.wait_ge(q["shift_ready"].handle, q["shift_ready"].at(g + 1))
                        if due(g):
                            ac.wait_ge(q["wide_ready"].handle, q["wide_ready"].at(g))
                        nc.scalar.activation(res[:], dif[:], ACT.Exp).then_inc(q["res_ready"].handle, 1)
                        ac.wait_ge(q["colsT_ready"].handle, q["colsT_ready"].at(g + 1))
                        if due(g):
                            ac.wait_ge(q["edge_ready"].handle, q["edge_ready"].at(g))
                        nc.scalar.activation(avm[:], small[0:WIN, 64:64 + 2 * H], ACT.Copy).then_inc(q["avm_ready"].handle, 1)

                    def distances(g, s, it):
                        ac.wait_ge(s_bA[s].handle, s_bA[s].at(it * 16 + 16))
                        ac.wait_ge(q["cols_ready"].handle, q["cols_ready"].at(g + 1))
                        for k in range(NSUB):
                            if has(g, 1):
                                ac.wait_ge(q["max_done"].handle, q["max_done"].at(NSUB * (g - 1) + k + 1))
                            nc.scalar.activation(far[k][:], bufA[s][:].bitcast(I32), ACT.Square, bias=subcol[:, k:k + 1],
                                                 scale=BIG).then_inc(q["far_ready"].handle, 1)

                    def weights(g, s):
                        ac.wait_ge(q["z_done"].handle, q["z_done"].at(g + 1))
                        if due(g - RG + 1):
                            ac.wait_ge(q["sum_ready"].handle, q["sum_ready"].at(g - RG + 1))
                        nc.scalar.activation(zpos[:], z[:], ACT.Relu).then_inc(q["zpos_ready"].handle, 1)
                        ac.wait_ge(q["zpos_ready"].handle, q["zpos_ready"].at(g + 1))
                        nc.scalar.activation(msg[s][:, :, D:ROW], zpos[:], ACT.Exp, scale=-1.0).then_inc(q["p_ready"].handle, 1)

                    def repeat(g, s, it):
                        ac.wait_ge(s_rows[s].handle, s_rows[s].at((it + 1) * 16 * G))
                        if due(g):
                            ac.wait_ge(q["scores_ready"].handle, q["scores_ready"].at(g))
                        ac.sem_inc(s_passed.handle, 1)
                        nc.scalar.activation(rep[:].rearrange("p j (a h) -> p j a h", h=H),
                                             bc(rows[s][:, :, D:ROW], [P, G, SUB, H], 2), ACT.Copy
                                             ).then_inc(q["rep_ready"].handle, 1)

                    def body(g, s, it):
                        if has(g, 1):
                            columns(g - 1)
                        if not (isinstance(g, int) and g == NG - 1):
                            distances(*following(g, s, it))
                            repeat(*following(g, s, it))
                        if has(g, 1):
                            weights(g - 1, (s - 1) % RG)
                    distances(0, 0, 0)
                    repeat(0, 0, 0)
                    turns(body, RG)(ac.Fori)
                    columns(NG - 1)
                    weights(NG - 1, (NG - 1) % RG)

                @block.vector
                def _(ve):
                    link = Chain(ve, s_ve)

                    def columns(g):
                        nc.vector.tensor_scalar(subcol[:], subnode[:], first[:, ds(g, 1)], -BIG, ALU.add, ALU.mult
                                                ).then_inc(q["cols_ready"].handle, 1)

                    def first_of(g):
                        return ve.value_load(first_i[0:1, ds(g, 1)], min_val=0, max_val=N)

                    def shifts(g, base):
                        m = xT[0:H, ds(base, WIN)]
                        a = auxT[0:H, ds(base, WIN)]
                        if due(g):
                            ve.wait_ge(q["colsT_ready"].handle, q["colsT_ready"].at(g))
                            ve.wait_ge(q["res_ready"].handle, q["res_ready"].at(g))
                        link.mark(nc.vector.tensor_tensor(U[:, 0, :], m, a, ALU.add))
                        link.mark(nc.vector.tensor_copy(adw[:], a))
                        link.join()
                        ve.wait_ge(q["winmax_ready"].handle, q["winmax_ready"].at(g + 1))
                        link(nc.vector.tensor_tensor(m, m, small[0:H, 0:WIN], ALU.max))
                        link(nc.vector.tensor_tensor(U[:, 1, :], m, a, ALU.add))
                        link(nc.vector.scalar_tensor_tensor(V[:], U[:], SLOPE, U[:], ALU.mult, ALU.max))
                        nc.vector.tensor_tensor(dif[:], V[:, 0, :], V[:, 1, :], ALU.subtract).then_inc(q["shift_ready"].handle, 1)

                    def maxima(g):
                        ve.wait_ge(q["scores_ready"].handle, q["scores_ready"].at(g + 1))
                        ve.sem_inc(s_passed.handle, 1)
                        for k in range(NSUB):
                            nc.vector.tensor_tensor_reduce(
                                out=far[k][:], in0=scores[:], in1=far[k][:], scale=1.0, scalar=-3.0e38, op0=ALU.subtract,
                                op1=ALU.max, accum_out=submax[:, k:k + 1]).then_inc(q["max_done"].handle, 1)

                    def body(g, s, it, real=True):
                        if real:
                            ve.wait_ge(q["far_ready"].handle, q["far_ready"].at(NSUB * (g + 1)))
                            if not (isinstance(g, int) and g == NG - 1):
                                columns(g + 1)
                            maxima(g)
                            base = first_of(g)
                        if has(g, 2):
                            base2 = first_of(g - 2)
                        if real:
                            ve.wait_ge(q["max_done"].handle, q["max_done"].at(NSUB * (g + 1)))
                            nc.vector.tensor_tensor(subpick[:], bc(submax[:], [P, NSUB, SUB], 2), bc(pick[:], [P, NSUB, SUB], 1),
                                                    ALU.mult).then_inc(q["pick_ready"].handle, 1)
                            if due(g - RG + 1):
                                ve.wait_ge(q["sum_ready"].handle, q["sum_ready"].at(g - RG + 1))
                            nc.vector.tensor_tensor(sel[s][:], bc(iota[:], [P, G, WIN], 1),
                                                    bc(drel[:, ds(g, 1), :].rearrange("p o j -> p (o j)"), [P, G, WIN], 2),
                                                    ALU.is_equal).then_inc(q["sel_ready"].handle, 1)
                        if has(g, 1):
                            before = (s - 1) % RG
                            ve.wait_ge(q["edge_ready"].handle, q["edge_ready"].at(g))
                            if due(g - 1):
                                ve.wait_ge(q["p_ready"].handle, q["p_ready"].at(g - 1))
                            ed = edge[:, 0:G * 2 * H].rearrange("p (j v) -> p j v", v=2 * H)
                            link(nc.vector.tensor_tensor(z[:], rows[before][:, :, D:ROW], ed[:, :, 0:H], ALU.add))
                            link(nc.vector.scalar_tensor_tensor(z[:], z[:], SLOPE, z[:], ALU.mult, ALU.max))
                            nc.vector.tensor_tensor(z[:], ed[:, :, H:2 * H], z[:], ALU.subtract).then_inc(q["z_done"].handle, 1)
                        if real:
                            ve.wait_ge(s_bA[s].handle, s_bA[s].at(it * 16 + 16))
                            if due(g - RG + 1):
                                ve.wait_ge(q["edge_ready"].handle, q["edge_ready"].at(g - RG + 1))
                            nc.vector.tensor_scalar(bufB[s][0:WIN, :], bufA[s][0:WIN, :].bitcast(I32), first[0:WIN, ds(g, 1)], part[0:WIN, :],
                                                    ALU.subtract, ALU.is_equal).then_inc(q["selT_ready"].handle, 1)
                        if has(g, 1):
                            ve.wait_ge(q["p_ready"].handle, q["p_ready"].at(g))
                            nc.vector.tensor_tensor(msg[before][:, :, 0:D].rearrange("p j (h c) -> p j h c", c=C),
                                                    rows[before][:, :, 0:D].rearrange("p j (h c) -> p j h c", c=C),
                                                    bc(msg[before][:, :, D:ROW], [P, G, H, C], 3), ALU.mult
                                                    ).then_inc(q["msg_ready"].handle, 1)
                        if has(g, 2):
                            add_sums(g - 2, (s - 2) % RG, base2)
                        if real:
                            shifts(g, base)

                    def add_sums(g, s, base):
                        w = accT[0:ROW, ds(base, WIN)]
                        ve.wait_ge(q["wide_ready"].handle, q["wide_ready"].at(g + 1))
                        ve.wait_ge(q["sum_ready"].handle, q["sum_ready"].at(g + 1))
                        if due(g):
                            ve.wait_ge(q["acc_done"].handle, q["acc_done"].at(g))
                        link(nc.vector.tensor_tensor(w, w, wide[s % 2][0:ROW, 64:64 + WIN], ALU.mult))
                        nc.vector.tensor_tensor(w, w, wide[s % 2][0:ROW, 0:WIN], ALU.add).then_inc(q["acc_done"].handle, 1)

                    columns(0)
                    body(0, 0, 0)
                    n0 = link.close()
                    link.offset = n0
                    body(1, 1, 0)
                    n1 = n0 + link.close()
                    link.offset = n1
                    body(2, 2, 0)
                    n2 = link.close()
                    for g in range(3, RG):
                        link.offset = n1 + n2 * (g - 2)
                        body(g, g, 0)
                        link.close()
                    with ve.Fori(1, NG // RG) as it:
                        for s in range(RG):
                            link.offset = n1 + n2 * (it * RG + s - 2)
                            body(it * RG + s, s, it)
                            assert link.close() == n2
                    for g in range(RG * (NG // RG), NG):
                        link.offset = n1 + n2 * (g - 2)
                        body(g, g % RG, g // RG)
                        link.close()
                    link.offset = n1 + n2 * (NG - 2)
                    body(NG, NG % RG, NG // RG, real=False)
                    add_sums(NG - 1, (NG - 1) % RG, first_of(NG - 1))
                    s_ve.total = link.offset + link.close()
            s_ve.done(s_ve.total)
            for s in range(RG):
                s_idx[s].done(16 * slot_total(s, RG))
                s_bA[s].done(16 * slot_total(s, RG))
            for n in ["avm_ready", "selT_ready", "z_done", "edge_ready", "sel_ready", "msg_ready", "sum_ready", "rep_ready",
                      "scores_ready", "pick_ready", "winmax_ready", "shift_ready", "colsT_ready", "res_ready",
                      "acc_done", "wide_ready", "zpos_ready", "p_ready", "cols_ready"]:
                q[n].done(NG)
            q["max_done"].done(NSUB * NG)
            q["far_ready"].done(NSUB * NG)
            gat_further(name)

        sum_pass("sage0", A["x"], attr=True, aux=True)
        sage_dense(0)
        sum_pass("sage1", node_table, attr=True)
        sage_dense(1)
        sum_pass("sage2", node_table, attr=True)
        sage_dense(2)
        sum_pass("gin0", node_table)
        gin_dense0()
        sum_pass("gin1", node_table)
        gin_dense1()
        gat_pass("gat0")
        gat_dense("1", "3")
        gat_pass("gat1")
        gat_dense("3", "2")
        gat_pass("gat2")
        gat_dense("2", None)


def constants():
    p = np.arange(P)
    f = np.float32
    c = {"c_ident": np.eye(P, dtype=f), "c_iota": np.tile(np.arange(WIN, dtype=f), (P, 1)), "c_part": p[:, None].astype(f)}
    c["c_subnode"] = (p[:, None] // H + SUB * np.arange(NSUB)[None]).astype(f)
    c["c_pick"] = (p[:, None] // H == np.arange(SUB)[None]).astype(f)
    c["c_heads"] = (p[:, None] % H == np.arange(H)[None]).astype(f)
    w = np.zeros((H, ROW), f)
    for h in range(H):
        w[h, h * C:(h + 1) * C] = 1
        w[h, D + h] = 1
    c["c_widen"] = w
    d = np.zeros((ROW, D), f)
    for h in range(H):
        d[D + h, h * C:(h + 1) * C] = 1
    c["c_denom"] = d
    c["c_blk"] = (np.arange(D)[:, None] // C == np.arange(H)[None]).astype(f)
    return c


def lay_out(inputs):
    a = {k: np.asarray(v) for k, v in inputs.items()}
    pad = lambda v, fill: np.concatenate([v, np.full((EP - E,) + v.shape[1:], fill, v.dtype)])
    o = constants()
    o["src"] = pad(a["src"], 0).reshape(NG, P, G)
    dst = pad(a["dst"], N).reshape(NG, P, G)
    o["dst"] = np.ascontiguousarray(dst.transpose(1, 0, 2)).reshape(P, NG * G)
    o["dst_rows"] = np.ascontiguousarray(dst.transpose(0, 2, 1)).reshape(NG, GE)
    o["wgt"] = np.ascontiguousarray(pad(a["edge_weight"], 0).reshape(NG, P, G).transpose(1, 0, 2))
    o["attr16"] = np.ascontiguousarray(pad(a["edge_attr_16"], 0).reshape(NG, P, G, EA).transpose(0, 3, 2, 1)).reshape(NG, EA, GE)
    o["attr64"] = pad(a["edge_attr_64"], 0).reshape(NG, P, G * D)
    o["x"] = np.concatenate([a["x"], np.zeros((NP - N, D), a["x"].dtype)])
    o["emb"] = a["L0_gnn_emb_ea"]
    for i in range(3):
        o[f"Wl{i}"], o[f"Wr{i}"] = a[f"L0_gnn_Wl{i}"], a[f"L0_gnn_Wr{i}"]
    for i in range(2):
        o[f"W1{i}"], o[f"W2{i}"] = a[f"L1_gnn_W1_{i}"].T, a[f"L1_gnn_W2_{i}"].T
    for k in "132":
        o["G" + k] = a["L3_gnn_W" + k].T
    c = [a["L0_gnn_bl0"], a["L0_gnn_bl1"], a["L0_gnn_bl2"], a["L3_gnn_b1"], a["L3_gnn_b3"], a["L3_gnn_b2"]]
    for k in "132":
        c += [a["L3_gnn_as" + k].reshape(D), a["L3_gnn_ad" + k].reshape(D)]
    o["cols"] = np.stack(c, 1)
    return {k: np.ascontiguousarray(v) for k, v in o.items()}


def kernel(**inputs):
    import concourse.bacc as bacc
    from concourse.bass_utils import run_bass_kernel_spmd

    nc = bacc.Bacc("TRN2", target_bir_lowering=False, num_devices=1)
    arrays = lay_out(inputs)
    aps = {k: nc.dram_tensor("in_" + k, v.shape, mybir.dt.from_np(v.dtype), kind="ExternalInput").ap()
           for k, v in arrays.items()}
    out = nc.dram_tensor("out", (N, D), F32, kind="ExternalOutput").ap()
    build(nc, aps, out)
    r = run_bass_kernel_spmd(nc, [{"in_" + k: v for k, v in arrays.items()}], core_ids=[0])
    return r.results[0]["out"]
```
